# Optimizing a Trainium2 kernel written in Bass

```python
import numpy as np
import jax
import jax.numpy as jnp

def _softmax(x, axis=-1):
    return jax.nn.softmax(x, axis=axis)

def _gelu(x):
    return jax.nn.gelu(x, approximate=True)

def _silu(x):
    return jax.nn.silu(x)

def _sigmoid(x):
    return jax.nn.sigmoid(x)

def _layernorm(x, axis=-1, eps=1e-05):
    m = jnp.mean(x, axis=axis, keepdims=True)
    v = jnp.var(x, axis=axis, keepdims=True)
    return (x - m) / jnp.sqrt(v + eps)

def _scatter_add(tgt, idx, src, axis=0):
    return tgt.at[idx].add(src)

def _segment_sum(src, seg, n):
    return jax.ops.segment_sum(src, seg, n)
kernel_name = 'mk_adaln_d2_jaxref_r8_c4432d'

def setup_inputs(seed: int=0):
    np.random.seed(seed)
    _w = jnp.asarray

    def _L0_attn_setup():
        import jax, jax.numpy as jnp
        import numpy as np
        INDIM = 128
        NHEADS = 16
        DK = INDIM // NHEADS
        DV = INDIM // NHEADS
        B, S = (4, 256)
        key = jax.random.key(seed)
        ks = jax.random.split(key, 5)
        x = jax.random.normal(ks[0], (B, S, INDIM), dtype=jnp.float32)
        std_qk = np.sqrt(2.0 / (INDIM + DK)).astype(np.float32)
        std_v = np.sqrt(2.0 / (INDIM + DV)).astype(np.float32)
        Wq = jax.random.normal(ks[1], (NHEADS * DK, INDIM), dtype=jnp.float32) * std_qk
        Wk = jax.random.normal(ks[2], (NHEADS * DK, INDIM), dtype=jnp.float32) * std_qk
        Wv = jax.random.normal(ks[3], (NHEADS * DV, INDIM), dtype=jnp.float32) * std_v
        std_o = np.sqrt(2.0 / (NHEADS * DV + INDIM)).astype(np.float32)
        Wo = jax.random.normal(ks[4], (INDIM, NHEADS * DV), dtype=jnp.float32) * std_o
        bq = jnp.zeros((NHEADS * DK,), jnp.float32)
        bk = jnp.zeros((NHEADS * DK,), jnp.float32)
        bv = jnp.zeros((NHEADS * DV,), jnp.float32)
        bo = jnp.zeros((INDIM,), jnp.float32)
        return {'x': x, 'Wq': Wq, 'bq': bq, 'Wk': Wk, 'bk': bk, 'Wv': Wv, 'bv': bv, 'Wo': Wo, 'bo': bo}
    _L0_attn_in = _L0_attn_setup()

    def _L0_ffn_setup():
        import jax, jax.numpy as jnp
        import numpy as np
        B, S, H = (2, 256, 128)
        N, F, SF, K = (16, 128, 512, 1)
        key = jax.random.key(seed)
        ks = jax.random.split(key, 7)
        std = 0.02
        return {'hidden_states': jax.random.normal(ks[0], (B, S, H), dtype=jnp.float32), 'router_w': jax.random.normal(ks[1], (N, H), dtype=jnp.float32) * std, 'gate_up_proj': jax.random.normal(ks[2], (N, H, 2 * F), dtype=jnp.float32) * std, 'down_proj': jax.random.normal(ks[3], (N, F, H), dtype=jnp.float32) * std, 'shared_gate_w': jax.random.normal(ks[4], (SF, H), dtype=jnp.float32) * std, 'shared_up_w': jax.random.normal(ks[5], (SF, H), dtype=jnp.float32) * std, 'shared_down_w': jax.random.normal(ks[6], (H, SF), dtype=jnp.float32) * std}
    _L0_ffn_in = _L0_ffn_setup()
    _L0_c = _w((lambda *s: np.random.randn(*s).astype(np.float32) * 0.05)(1, 128))
    _L0_wmod = _w((lambda *s: np.random.randn(*s).astype(np.float32) * 0.05)(128, 6 * 128) * 128 ** (-0.5))

    def _L1_attn_setup():
        import jax, jax.numpy as jnp
        import numpy as np
        B, T, C = (4, 256, 128)
        NQ, D = (8, C // 8)
        key = jax.random.key(seed)
        ks = jax.random.split(key, 6)
        s = 0.02
        return {'x': jax.random.normal(ks[0], (B, T, C), dtype=jnp.float32), 'Wk': jax.random.normal(ks[1], (C, D), dtype=jnp.float32) * s, 'Wv': jax.random.normal(ks[2], (C, D), dtype=jnp.float32) * s, 'Wq': jax.random.normal(ks[3], (NQ, C, D), dtype=jnp.float32) * s, 'Wp': jax.random.normal(ks[4], (NQ * D, C), dtype=jnp.float32) * s, 'bp': jnp.zeros((C,), dtype=jnp.float32)}
    _L1_attn_in = _L1_attn_setup()

    def _L1_ffn_setup():
        import jax, jax.numpy as jnp
        import numpy as np
        DIM = 128

        def _reference_tuple_inner(x, W_r, W_k, W_v, mu_r, mu_k):
            B, T, C = x.shape
            x_prev = jnp.concatenate([jnp.zeros((B, 1, C), x.dtype), x[:, :-1, :]], axis=1)
            xr = mu_r * x + (1.0 - mu_r) * x_prev
            xk = mu_k * x + (1.0 - mu_k) * x_prev
            r = jax.nn.sigmoid(jnp.einsum('btc,dc->btd', xr, W_r))
            k = jnp.einsum('btc,dc->btd', xk, W_k)
            k_act = jnp.square(jax.nn.relu(k))
            out = r * jnp.einsum('btc,dc->btd', k_act, W_v)
            new_state = x[:, -1, :]
            return (out, new_state)
        key = jax.random.key(seed)
        ks = jax.random.split(key, 6)
        B, T, C = (8, 256, DIM)
        x = jax.random.normal(ks[0], (B, T, C), dtype=jnp.float32)
        s = 1.0 / np.sqrt(C)
        W_r = jax.random.uniform(ks[1], (C, C), jnp.float32, -s, s)
        W_k = jax.random.uniform(ks[2], (C, C), jnp.float32, -s, s)
        W_v = jax.random.uniform(ks[3], (C, C), jnp.float32, -s, s)
        mu_r = jax.random.uniform(ks[4], (C,), jnp.float32)
        mu_k = jax.random.uniform(ks[5], (C,), jnp.float32)
        return {'x': x, 'W_r': W_r, 'W_k': W_k, 'W_v': W_v, 'mu_r': mu_r, 'mu_k': mu_k}
    _L1_ffn_in = _L1_ffn_setup()
    _L1_c = _w((lambda *s: np.random.randn(*s).astype(np.float32) * 0.05)(1, 128))
    _L1_wmod = _w((lambda *s: np.random.randn(*s).astype(np.float32) * 0.05)(128, 6 * 128) * 128 ** (-0.5))
    _d = {'L0_attn_x': _L0_attn_in['x'], 'L0_attn_Wq': _L0_attn_in['Wq'], 'L0_attn_bq': _L0_attn_in['bq'], 'L0_attn_Wk': _L0_attn_in['Wk'], 'L0_attn_bk': _L0_attn_in['bk'], 'L0_attn_Wv': _L0_attn_in['Wv'], 'L0_attn_bv': _L0_attn_in['bv'], 'L0_attn_Wo': _L0_attn_in['Wo'], 'L0_attn_bo': _L0_attn_in['bo'], 'L0_ffn_router_w': _L0_ffn_in['router_w'], 'L0_ffn_gate_up_proj': _L0_ffn_in['gate_up_proj'], 'L0_ffn_down_proj': _L0_ffn_in['down_proj'], 'L0_ffn_shared_gate_w': _L0_ffn_in['shared_gate_w'], 'L0_ffn_shared_up_w': _L0_ffn_in['shared_up_w'], 'L0_ffn_shared_down_w': _L0_ffn_in['shared_down_w'], 'L0_c': _L0_c, 'L0_wmod': _L0_wmod, 'L1_attn_Wk': _L1_attn_in['Wk'], 'L1_attn_Wv': _L1_attn_in['Wv'], 'L1_attn_Wq': _L1_attn_in['Wq'], 'L1_attn_Wp': _L1_attn_in['Wp'], 'L1_attn_bp': _L1_attn_in['bp'], 'L1_ffn_W_r': _L1_ffn_in['W_r'], 'L1_ffn_W_k': _L1_ffn_in['W_k'], 'L1_ffn_W_v': _L1_ffn_in['W_v'], 'L1_ffn_mu_r': _L1_ffn_in['mu_r'], 'L1_ffn_mu_k': _L1_ffn_in['mu_k'], 'L1_c': _L1_c, 'L1_wmod': _L1_wmod}
    _x0 = _d['L0_attn_x']
    _d['L0_attn_x'] = jax.random.normal(jax.random.fold_in(jax.random.key(seed), 1), (1, 2048, 128), dtype=_x0.dtype)
    del _x0
    return _d

def reference(L0_attn_x, L0_attn_Wq, L0_attn_bq, L0_attn_Wk, L0_attn_bk, L0_attn_Wv, L0_attn_bv, L0_attn_Wo, L0_attn_bo, L0_ffn_router_w, L0_ffn_gate_up_proj, L0_ffn_down_proj, L0_ffn_shared_gate_w, L0_ffn_shared_up_w, L0_ffn_shared_down_w, L0_c, L0_wmod, L1_attn_Wk, L1_attn_Wv, L1_attn_Wq, L1_attn_Wp, L1_attn_bp, L1_ffn_W_r, L1_ffn_W_k, L1_ffn_W_v, L1_ffn_mu_r, L1_ffn_mu_k, L1_c, L1_wmod):

    def _L0_attn_ref(x, Wq, bq, Wk, bk, Wv, bv, Wo, bo):
        import jax, jax.numpy as jnp
        import numpy as np
        INDIM = 128
        NHEADS = 16
        DK = INDIM // NHEADS
        DV = INDIM // NHEADS
        B, S = (4, 256)
        b, s, _ = x.shape
        q = (x @ Wq.T + bq).reshape(b, s, NHEADS, DK)
        k = (x @ Wk.T + bk).reshape(b, s, NHEADS, DK)
        v = (x @ Wv.T + bv).reshape(b, s, NHEADS, DV)
        w = jnp.einsum('bshd,bzhd->bhsz', q, k)
        w = w / jnp.sqrt(jnp.float32(DV))
        w = jax.nn.softmax(w, axis=-1)
        vw = jnp.einsum('bhsz,bzhd->bshd', w, v)
        vw = vw.reshape(b, s, NHEADS * DV)
        out = vw @ Wo.T + bo
        return out

    def _L0_ffn_ref(hidden_states, router_w, gate_up_proj, down_proj, shared_gate_w, shared_up_w, shared_down_w):
        import jax, jax.numpy as jnp
        import numpy as np
        B, S, H = (2, 256, 128)
        N, F, SF, K = (16, 128, 512, 1)
        b, s, h = hidden_states.shape
        hidden = hidden_states.reshape(-1, h)
        t = hidden.shape[0]
        logits = hidden @ router_w.T
        top_vals, top_idx = jax.lax.top_k(logits, K)
        scores = jnp.full_like(logits, -jnp.inf)
        scores = scores.at[jnp.arange(t)[:, None], top_idx].set(top_vals)
        scores = jax.nn.sigmoid(scores.astype(jnp.float32)).astype(hidden.dtype)
        routed_in = hidden[None, :, :] * scores.T[:, :, None]
        gate_up = jnp.einsum('nth,nhf->ntf', routed_in, gate_up_proj)
        gate, up = jnp.split(gate_up, 2, axis=-1)
        routed_out = jnp.einsum('ntf,nfh->nth', up * jax.nn.silu(gate), down_proj)
        expert_sum = routed_out.sum(axis=0)
        shared = jax.nn.silu(hidden @ shared_gate_w.T) * (hidden @ shared_up_w.T) @ shared_down_w.T
        return (shared + expert_sum).reshape(b, s, h)

    def _L1_attn_ref(x, Wk, Wv, Wq, Wp, bp):
        import jax, jax.numpy as jnp
        import numpy as np
        B, T, C = (4, 256, 128)
        NQ, D = (8, C // 8)
        b, t, c = x.shape
        scale = c ** (-0.5)
        k = x @ Wk
        v = x @ Wv
        q = jnp.einsum('btc,qcd->bqtd', x, Wq)
        wei = jnp.einsum('bqtd,bsd->bqts', q, k) * scale
        causal = jnp.tril(jnp.ones((t, t), dtype=bool))
        wei = jnp.where(causal, wei, -jnp.inf)
        wei = jax.nn.softmax(wei, axis=-1)
        out = jnp.einsum('bqts,bsd->btqd', wei, v)
        out = out.reshape(b, t, -1)
        return out @ Wp + bp

    def _L1_ffn_ref(x, W_r, W_k, W_v, mu_r, mu_k):
        import jax, jax.numpy as jnp
        import numpy as np
        DIM = 128

        def _reference_tuple_inner(x, W_r, W_k, W_v, mu_r, mu_k):
            B, T, C = x.shape
            x_prev = jnp.concatenate([jnp.zeros((B, 1, C), x.dtype), x[:, :-1, :]], axis=1)
            xr = mu_r * x + (1.0 - mu_r) * x_prev
            xk = mu_k * x + (1.0 - mu_k) * x_prev
            r = jax.nn.sigmoid(jnp.einsum('btc,dc->btd', xr, W_r))
            k = jnp.einsum('btc,dc->btd', xk, W_k)
            k_act = jnp.square(jax.nn.relu(k))
            out = r * jnp.einsum('btc,dc->btd', k_act, W_v)
            new_state = x[:, -1, :]
            return (out, new_state)
        return _reference_tuple_inner(x, W_r, W_k, W_v, mu_r, mu_k)[0]
    x = L0_attn_x
    mod = (_silu(L0_c) @ L0_wmod).reshape(L0_c.shape[0], 6, 1, -1)
    sa, ca, ga, sb, cb, gb = (mod[:, 0], mod[:, 1], mod[:, 2], mod[:, 3], mod[:, 4], mod[:, 5])
    ga = (2 * (ga >= 0) - 1) * jnp.maximum(jnp.abs(ga), 0.25)
    gb = (2 * (gb >= 0) - 1) * jnp.maximum(jnp.abs(gb), 0.25)
    h = _layernorm(x, axis=-1) * (1 + ca) + sa
    x = x + ga * _L0_attn_ref(h, L0_attn_Wq, L0_attn_bq, L0_attn_Wk, L0_attn_bk, L0_attn_Wv, L0_attn_bv, L0_attn_Wo, L0_attn_bo)
    h = _layernorm(x, axis=-1) * (1 + cb) + sb
    x = x + gb * _L0_ffn_ref(h, L0_ffn_router_w, L0_ffn_gate_up_proj, L0_ffn_down_proj, L0_ffn_shared_gate_w, L0_ffn_shared_up_w, L0_ffn_shared_down_w)
    mod = (_silu(L1_c) @ L1_wmod).reshape(L1_c.shape[0], 6, 1, -1)
    sa, ca, ga, sb, cb, gb = (mod[:, 0], mod[:, 1], mod[:, 2], mod[:, 3], mod[:, 4], mod[:, 5])
    ga = (2 * (ga >= 0) - 1) * jnp.maximum(jnp.abs(ga), 0.25)
    gb = (2 * (gb >= 0) - 1) * jnp.maximum(jnp.abs(gb), 0.25)
    h = _layernorm(x, axis=-1) * (1 + ca) + sa
    x = x + ga * _L1_attn_ref(h, L1_attn_Wk, L1_attn_Wv, L1_attn_Wq, L1_attn_Wp, L1_attn_bp)
    h = _layernorm(x, axis=-1) * (1 + cb) + sb
    x = x + gb * _L1_ffn_ref(h, L1_ffn_W_r, L1_ffn_W_k, L1_ffn_W_v, L1_ffn_mu_r, L1_ffn_mu_k)
    return x

_drawn_inputs = setup_inputs


def setup_inputs(seed=0):
    import zlib

    import numpy as np

    out = dict(_drawn_inputs(seed))
    spreads = {'L0_attn_bq': (0.0, 0.8),
     'L0_attn_bk': (0.0, 2.0),
     'L0_attn_bv': (0.0, 0.344),
     'L0_attn_bo': (0.0, 0.325),
     'L1_attn_bp': (0.0, 1.227)}
    factors = {'L0_ffn_router_w': 8.0,
     'L0_ffn_gate_up_proj': 8.0,
     'L0_ffn_down_proj': 8.0,
     'L0_ffn_shared_gate_w': 8.0,
     'L0_ffn_shared_up_w': 8.0,
     'L0_ffn_shared_down_w': 8.0,
     'L1_attn_Wk': 8.0,
     'L1_attn_Wv': 8.0,
     'L1_attn_Wq': 8.0,
     'L1_attn_Wp': 8.0,
     'L1_ffn_W_r': 8.0,
     'L1_ffn_W_k': 2.967,
     'L1_ffn_W_v': 2.759,
     'L1_ffn_mu_r': 8.0,
     'L1_ffn_mu_k': 4.663}
    for name, (base, spread) in spreads.items():
        noise = np.random.default_rng([zlib.crc32(name.encode()), seed]).standard_normal(out[name].shape)
        drawn = base * np.exp(spread * noise) if base else spread * noise
        out[name] = jnp.asarray(drawn.astype(out[name].dtype))
    for name, factor in factors.items():
        out[name] = (out[name] * factor).astype(out[name].dtype)
    return out
```

```python
import concourse.bass as bass
from concourse import mybir
from contextlib import ExitStack

F32 = mybir.dt.float32
BF16 = mybir.dt.bfloat16
ALU = mybir.AluOpType
ACT = mybir.ActivationFunctionType
AX = mybir.AxisListType

S = 2048
NC_ = 4
CH = 512
EPS = 1e-5
NEG = -1e30


def adaln_two_layers(nc, A, out):
    ctx = ExitStack()
    with ctx:
        def sb(name, shape, dt=F32):
            return ctx.enter_context(nc.sbuf_tensor(name, shape, dt))

        def pb(name, shape):
            return ctx.enter_context(nc.psum_tensor(name, shape, F32))

        queues = {"pe": [], "dv": [], "ac": [], "po": [], "sp": []}
        sems, counts = {}, {}

        def sem(name):
            if name not in sems:
                sems[name] = ctx.enter_context(nc.semaphore(name))
                counts[name] = 0
            return sems[name]

        def add(eng, fn, sig=None, after=(), by=1):
            tok = None
            if sig is not None:
                sem(sig)
                counts[sig] += by
                tok = (sig, counts[sig])
            queues[eng].append((fn, sig, by, [t for t in after if t is not None]))
            return tok

        def dma(dst, src, sig, after=(), eng="sp"):
            return add(eng, lambda e: e.dma_start(dst, src), sig, after, by=16)

        def run(name, e):
            seen = {}
            for fn, sig, by, after in queues[name]:
                for s, v in after:
                    if seen.get(s, 0) < v:
                        e.wait_ge(sems[s], v)
                        seen[s] = v
                ins = fn(e)
                if sig is not None:
                    ins.then_inc(sems[sig], by)

        Qs = sb("Qs", [128, 8, S], BF16)
        Ks = sb("Ks", [128, 8, S], BF16)
        Va = sb("Va", [128, 16, 16, 32])
        V1 = sb("V1", [128, 16, 32])
        xs = sb("xs", [128, 16, 128])
        hT = sb("hT", [128, 1 + S])
        xh = sb("xh", [128, 8, 128])
        PT = [sb(f"PT{i}", [128, 1024]) for i in range(4)]
        qf = sb("qf", [128, 2, CH])
        q3 = sb("q3", [128, 2, 3, CH], BF16)
        st = sb("st", [128, 16, 6])
        mv = sb("mv", [128, 16, 2])
        ve = sb("ve", [128, 16])
        rs = sb("rs", [128, 16])
        mh = sb("mh", [128, 4])
        ones3 = PT[3][0:3, :].bitcast(BF16)
        Os = sb("Os", [128, 2, CH])
        rl = sb("rl", [128, 16, 16])
        vw = sb("vw", [128, 2, 4, 128])
        vwT = sb("vwT", [128, 2, CH])
        mxr = sb("mx", [128, 1024])
        mx = mxr[:, :].rearrange("p (u q k) -> p u q k", u=16, k=4)
        nm = sb("nm", [128, 16, 16])
        nr = sb("nr", [128, 16, 16])
        n3 = sb("n3", [128, 16, 4, 4, 3], BF16)
        nrow = sb("nrow", [12, 2, CH], BF16)
        idf = sb("idf", [128, 128])
        idb = sb("idb", [128, 128], BF16)
        mq = sb("mq", [128, 128], BF16)
        mk = sb("mk", [128, 128], BF16)
        E = mxr[0:16, :].bitcast(BF16).rearrange("p (n m) -> p n m", n=16)
        onesf = sb("onesf", [128, 128])
        wqT, wkT, wvT, woT = (sb(n, [128, 128]) for n in ("wqT", "wkT", "wvT", "woT"))
        bq, bk, bqs = (sb(n, [128, 1]) for n in ("bq", "bk", "bqs"))
        bvB, boB, bpB = (sb(n, [128, 128]) for n in ("bvB", "boB", "bpB"))
        rwT = sb("rwT", [128, 16])
        gu = sb("gu", [128, 16, 256])
        dn = sb("dn", [128, 16, 128])
        sgT, suT = sb("sgT", [128, CH]), sb("suT", [128, CH])
        sdT = sb("sdT", [128, 4, 128])
        wk1, wv1 = sb("wk1", [128, 16]), sb("wv1", [128, 16])
        wq1 = sb("wq1", [128, 128])
        wp1 = sb("wp1", [128, 128])
        wr, wkk, wvv = (sb(n, [128, 128]) for n in ("wr", "wkk", "wvv"))
        mur, muk, omr, omk = (sb(n, [128, 1]) for n in ("mur", "muk", "omr", "omk"))
        desc = sb("desc", [128, 16])
        mods = []
        cc = sb("cc", [128, 2])
        csg = sb("csg", [128, 2])
        cs = sb("cs", [128, 2])
        cb = PT[1][:, 768:1024].rearrange("p (i n) -> p i n", i=2)
        mc = sb("mc", [128, 2, 4])
        gB = sb("gB", [128, 4, 128])
        gt = PT[2][:, :].rearrange("p (a g n) -> p a g n", a=2, g=4)
        lg, eq, wv_, oh = (nm[:, 4 * i:4 * i + 4, :] for i in range(4))
        soh = nr[:, 0:4, :]
        ohb = sb("ohb", [128, 4, 16], BF16)
        lm, wm, sgm = (sb(n, [128, 4]) for n in ("lm", "wm", "sgm"))
        sT = vw[0:16, 0, :, :].rearrange("p t n -> p (t n)")
        ohT = vw[0:16, 1, :, :].rearrange("p t n -> p (t n)").bitcast(BF16)[:, 0:CH]

        At = [pb("At0", [128, 1024]), pb("At1", [128, 1024])]
        Sb = [pb("Sb0", [128, CH]), pb("Sb1", [128, CH])]
        Ob = pb("Ob", [128, CH])
        Mb = pb("Mb", [128, CH])
        A0, A1, A2, A3 = (At[i // 2][:, CH * (i % 2):CH * (i % 2) + CH] for i in range(4))

        dq = [nc.dram_tensor(f"split_{n}", [3, 128, S], BF16).ap() for n in "qk"]
        dq1 = nc.dram_tensor("split_q1", [3, 128, S], BF16).ap()
        dk1 = nc.dram_tensor("split_k1", [3, 16, S], BF16).ap()

        xd = A["L0_attn_x"].rearrange("a (t p) n -> p (a t) n", p=128)
        lx = [dma(xs[:, 4 * c:4 * c + 4, :], xd[:, 4 * c:4 * c + 4, :], f"ld_x{c}") for c in range(4)]
        dma(cc[:, 0:1], A["L0_c"].rearrange("a n -> n a"), "ld_c", eng="ac")
        lc = dma(cc[:, 1:2], A["L1_c"].rearrange("a n -> n a"), "ld_c", eng="ac")
        wm_sb = [PT[0], PT[1]]
        lw = None
        for i in range(2):
            lw = dma(wm_sb[i][:, 0:768], A[f"L{i}_wmod"], "ld_wm", eng="ac")
        def col(v):
            return v.rearrange("(n a) -> n a", a=1)
        for dst, src in ((wqT, A["L0_attn_Wq"]), (wkT, A["L0_attn_Wk"]), (wvT, A["L0_attn_Wv"])):
            l0 = dma(dst[:, :], src, "ld_w0")
        for dst, src in ((bq, "L0_attn_bq"), (bk, "L0_attn_bk")):
            l0 = dma(dst[:, :], col(A[src]), "ld_w0")
        l0 = dma(bvB[:, :], A["L0_attn_bv"].partition_broadcast(128), "ld_w0")
        for dst, src in ((woT[:, :], A["L0_attn_Wo"]),
                         (boB[:, :], A["L0_attn_bo"].partition_broadcast(128)),
                         (bpB[:, :], A["L1_attn_bp"].partition_broadcast(128)),
                         (rwT[:, :], A["L0_ffn_router_w"]),
                         (gu[:, :, :], A["L0_ffn_gate_up_proj"].rearrange("n h f -> h n f")),
                         (dn[:, :, :], A["L0_ffn_down_proj"].rearrange("n f h -> f n h")),
                         (sgT[:, :], A["L0_ffn_shared_gate_w"]), (suT[:, :], A["L0_ffn_shared_up_w"]),
                         (sdT[:, :, :], A["L0_ffn_shared_down_w"].rearrange("(b f) h -> f b h", f=128)),
                         (wk1[:, :], A["L1_attn_Wk"]), (wv1[:, :], A["L1_attn_Wv"]),
                         (wq1[:, :].rearrange("c (q d) -> c q d", q=8), A["L1_attn_Wq"].rearrange("q c d -> c q d")),
                         (wp1[:, :], A["L1_attn_Wp"]),
                         (wr[:, :], A["L1_ffn_W_r"]), (wkk[:, :], A["L1_ffn_W_k"]), (wvv[:, :], A["L1_ffn_W_v"]),
                         (mur[:, :], col(A["L1_ffn_mu_r"])), (muk[:, :], col(A["L1_ffn_mu_k"]))):
            l1 = dma(dst, src, "ld_w1")

        add("po", lambda e: e.memset(idf[:, :], 0.0), "c0")
        add("po", lambda e: e.memset(mq[:, :], 0.0), "c0")
        c0 = add("po", lambda e: e.memset(mk[:, :], 0.0), "c0")
        t_id = add("po", lambda e: e.affine_select(out=idf[:, :], in_=idf[:, :], compare_op=ALU.not_equal, fill=1.0,
                                                   base=0, pattern=[[-1, 128]], channel_multiplier=1), "c1", [c0])
        t_rs0 = None
        c1 = add("po", lambda e: e.affine_select(out=mq[:, :], in_=mq[:, :], compare_op=ALU.is_ge, fill=NEG,
                                                 base=0, pattern=[[-1, 128]], channel_multiplier=1), "c1")
        c1 = add("po", lambda e: e.affine_select(out=mk[:, :], in_=mk[:, :], compare_op=ALU.is_ge, fill=NEG,
                                                 base=0, pattern=[[1, 128]], channel_multiplier=-1), "c1")
        t_idb = add("po", lambda e: e.tensor_copy(idb[:, :], idf[:, :]), "c1", [t_id])
        add("po", lambda e: e.memset(mh[:, :], -0.5), "c1")
        c1 = add("po", lambda e: e.memset(ones3, 1.0), "c1")
        add("po", lambda e: e.memset(hT[:, 0:1], 0.0), "c1")
        t_one = c1
        add("dv", lambda e: e.memset(onesf[:, :], 1.0), "c2")
        t_va = add("dv", lambda e: e.memset(Va[:, :, :, :], 1.0), "c2")
        t_v1 = add("dv", lambda e: e.memset(V1[:, :, :], 1.0), "c2")
        for n in range(16):
            c2 = add("dv", lambda e, n=n: e.memset(desc[:, n:n + 1], float(16 - n)), "c2")
        for par in range(2):
            t_k1 = dma(Ks[64 * par + 48:64 * par + 51, :, :],
                       ones3.unsqueeze(1).to_broadcast([3, 8, S]), "ld_ones", [t_one])

        t = add("ac", lambda e: e.activation(csg[:, :], cc[:, :], ACT.Sigmoid), "ac_set", [lc])
        t = add("dv", lambda e: e.tensor_tensor(cs[:, :], cc[:, :], csg[:, :], ALU.mult), "dv_set", [t, lc])
        for i in range(2):
            tcb = add("dv", lambda e, i=i: e.tensor_scalar(cb[:, i, :], onesf[:, :], cs[:, i:i + 1], None, ALU.mult),
                      "dv_set", [t, c2])
        for i in range(2):
            for k, j in enumerate((0, 1, 3, 4)):
                tm = add("pe", lambda e, i=i, j=j, k=k: e.matmul(Ob[:, 4 * i + k:4 * i + k + 1],
                         wm_sb[i][:, 128 * j:128 * j + 128], cs[:, i:i + 1], start=True, stop=True),
                         "pe_set", [lw, tcb])
        tmc = add("dv", lambda e: e.tensor_copy(mc[:, :, :], Ob[:, 0:8].rearrange("p (i k) -> p i k", i=2)), "dv_set", [tm])
        tmc = add("dv", lambda e: e.tensor_scalar(mc[:, :, 1:4:2], mc[:, :, 1:4:2], 1.0, None, ALU.add), "dv_set", [tmc])
        for i in range(2):
            for k, j in enumerate((2, 5)):
                g = 2 * i + k
                tm = add("pe", lambda e, i=i, j=j, g=g: e.matmul(Mb[:, 128 * g:128 * g + 128],
                         cb[:, i, :], wm_sb[i][:, 128 * j:128 * j + 128], start=True, stop=True), "pe_set")
        Mv = Mb[:, :].rearrange("p (g n) -> p g n", g=4)
        t1 = add("dv", lambda e: e.tensor_scalar(gt[:, 0, :, :], Mv, 0.0, 2.0, ALU.is_ge, ALU.mult), "dv_set", [tm])
        gf = gB[:, :, :].rearrange("p g n -> p (g n)")
        t2 = add("dv", lambda e: e.tensor_copy(gf, Mb[:, :]), "dv_set")
        free = {"M": t2, "O": tmc, "S0": None, "S1": None, "A0": None, "A1": None}
        t2 = add("dv", lambda e: e.scalar_tensor_tensor(PT[2][:, CH:], gf, -1.0, gf, ALU.mult, ALU.max), "dv_set", [t2])
        t2 = add("dv", lambda e: e.tensor_scalar(PT[2][:, CH:], PT[2][:, CH:], 0.25, None, ALU.max), "dv_set", [t2])
        tg = add("dv", lambda e: e.scalar_tensor_tensor(gB[:, :, :].rearrange("p g n -> p (g n)"), PT[2][:, 0:CH], -1.0,
                                                        PT[2][:, CH:], ALU.add, ALU.mult), "dv_set", [t2])
        tbq = add("dv", lambda e: e.tensor_scalar(bqs[:, :], bq[:, :], 8.0 ** -0.5, None, ALU.mult), "dv_set", [l0])
        def scale_w(w, g):
            return add("po", lambda e: e.tensor_tensor(w[:, :], w[:, :], gB[:, g, :], ALU.mult), "po_set", [tg, l1])
        t_wo = scale_w(woT, 0)
        scale_w(boB, 0)
        scale_w(bpB, 2)
        t_wp = scale_w(wp1, 2)
        t_wvv = scale_w(wvv, 3)
        add("po", lambda e: e.tensor_tensor(dn[:, :, :], dn[:, :, :], gB[:, 1, :].unsqueeze(1).to_broadcast([128, 16, 128]), ALU.mult), "po_set")
        t_dn = add("po", lambda e: e.tensor_tensor(sdT[:, :, :], sdT[:, :, :], gB[:, 1, :].unsqueeze(1).to_broadcast([128, 4, 128]), ALU.mult), "po_set")
        add("dv", lambda e: e.tensor_scalar(omr[:, :], mur[:, :], -1.0, 1.0, ALU.mult, ALU.add), "dv_om", [l1])
        t_om = add("dv", lambda e: e.tensor_scalar(omk[:, :], muk[:, :], -1.0, 1.0, ALU.mult, ALU.add), "dv_om")

        xh_tok = [None, None]

        def ln(c, layer, second, bank, bkey, x_ready, hT_free, tag, xh_free=None):
            xh_free = xh_tok[c % 2]
            k = 2 if second else 0
            for t_ in range(4 * c, 4 * c + 4):
                a = add("dv", lambda e, t_=t_: e.bn_stats(st[:, t_, :], xs[:, t_, :]), "dv_ln", [x_ready])
            for t_ in range(4 * c, 4 * c + 4):
                a = add("dv", lambda e, t_=t_: e.bn_aggr(mv[:, t_, :], st[:, t_, :]), "dv_ln", [a])
            cs_ = slice(4 * c, 4 * c + 4)
            b = add("po", lambda e: e.tensor_scalar(ve[:, cs_], mv[:, cs_, 1], EPS, None, ALU.add), "po_ln", [a])
            b = add("po", lambda e: e.tensor_tensor(rs[:, cs_], ve[:, cs_], mh[:, :], ALU.pow), "po_ln", [b, t_one])
            for t_ in range(4 * c, 4 * c + 4):
                d = add("dv", lambda e, t_=t_: e.tensor_scalar(xh[:, t_ % 8, :], xs[:, t_, :], mv[:, t_, 0:1], rs[:, t_:t_ + 1],
                                                               ALU.subtract, ALU.mult), "dv_xh", [b, xh_free])
            for j in range(4):
                p = add("pe", lambda e, j=j: e.transpose(bank[:, 128 * j:128 * j + 128], xh[:, (4 * c + j) % 8, :], idf[:, :]),
                        "pe_ln", [d, free[bkey], t_id])
            f = add("ac", lambda e: e.activation(hT[:, 1 + CH * c:1 + CH * c + CH], bank, ACT.Identity,
                                                 bias=mc[:, layer, k:k + 1], scale=mc[:, layer, k + 1:k + 2]),
                    "ac_h", [p, hT_free, tmc])
            free[bkey] = f
            xh_tok[c % 2] = p
            return f, p

        def hc(c, a=0, b=CH):
            return hT[:, 1 + CH * c + a:1 + CH * c + b]

        split_state = {"n": 0, "wr": [None, None]}

        def split(bank, bkey, ready, rows, bias, scale, dst):
            n = split_state["n"]
            split_state["n"] += 1
            s = n % 2
            prev = split_state["wr"][s]
            f = qf[0:rows, s, :]
            if bias is None:
                a = add("ac", lambda e: e.activation(f, bank[0:rows, :], ACT.Copy, scale=scale), "ac_sp", [ready, prev])
            else:
                a = add("ac", lambda e: e.activation(f, bank[0:rows, :], ACT.Identity, bias=bias, scale=scale), "ac_sp", [ready, prev, tbq])
            free[bkey] = a
            p = [q3[0:rows, s, i, :] for i in range(3)]
            b = add("ac", lambda e: e.activation(p[0], f, ACT.Copy), "ac_sp", [a])
            r = add("po", lambda e: e.tensor_tensor(f, f, p[0], ALU.subtract), "po_sp", [b])
            d = add("dv", lambda e: e.tensor_copy(p[1], f), "dv_sp", [r])
            g = add("po", lambda e: e.tensor_tensor(p[2], f, p[1], ALU.subtract), "po_sp", [d])
            w = dma(dst.rearrange("s p n -> p s n"), q3[0:rows, s, :, :], f"spw{n}", [g])
            split_state["wr"][s] = w
            return w

        QP, KP = (0, 0, 1, 1, 0, 2), (0, 1, 0, 1, 2, 0)

        t_q, t_k, t_v = [], [], []
        hts = []
        for c in range(4):
            h, xp = ln(c, 0, False, Mb[:, :], "M", lx[c], None, f"a{c}")
            hts.append((h, xp))
            for which, (w, bias, scale, key, bank) in enumerate((
                    (wkT, bk, 1.0, "S1", Sb[1]), (wqT, bqs, 8.0 ** -0.5, "S0", Sb[0]))):
                p = add("pe", lambda e, w=w, bank=bank, c=c: e.matmul(bank[:, :], w[:, :], hc(c), start=True, stop=True),
                        "pe_pr", [h, free[key], l0])
                cols = slice(CH * c, CH * c + CH)
                d_ = dq[1 - which]
                tw = split(bank, key, p, 128, bias[:, :], scale, d_[:, :, cols])
                slab = (Ks, Qs)[which]
                for par in range(2):
                    for j in range(6):
                        part = (KP, QP)[which][j]
                        src = d_[part].rearrange("(pr two d) n -> two d pr n", two=2, d=8)[par][:, :, cols]
                        tl = dma(slab[64 * par + 8 * j:64 * par + 8 * j + 8, :, cols], src, f"sl{which}{c}", [tw])
                (t_k, t_q)[which].append(tl)
            for j in range(4):
                p = add("pe", lambda e, c=c, j=j: e.matmul(Ob[:, 128 * j:128 * j + 128], hc(c, 128 * j, 128 * j + 128), wvT[:, :],
                                                           start=True, stop=True), "pe_pr", [free["O"]])
            for j in range(4):
                t = add("dv", lambda e, c=c, j=j: e.tensor_tensor(
                    Va[:, 4 * c + j, :, 0:8], Ob[:, 128 * j:128 * j + 128].rearrange("p (h d) -> p h d", d=8),
                    bvB[:, :].rearrange("p (h d) -> p h d", d=8), ALU.add), "dv_v", [p, t_va, l0])
            free["O"] = t
            t_v.append(t)
        xp_last = xp
        for c in range(4):
            t_xb = add("po", lambda e, c=c: e.tensor_tensor(xs[:, 4 * c:4 * c + 4, :], xs[:, 4 * c:4 * c + 4, :],
                       boB[:, :].unsqueeze(1).to_broadcast([128, 4, 128]), ALU.add), "po_xb", [hts[c][1], t_dn])

        def attention(L, units, smm, stmm, vmm, width, dcols, d_ready, shift_dst, wout, t_wout, x_ready, s_ready, st_ready):
            nU = len(units)
            steps = [(u, kt) for u in range(nU) for kt in range(width(u, None))]
            stiles = []
            for u in range(nU):
                stiles += [(u,) + x for x in smm(u, None)]
            n_of = [width(u, None) for u in range(nU)]
            tag = f"L{L}"
            state = {"si": 0}
            later = {}
            shift = [None] * nU
            x_done = {}
            sfree = [free["S0"], free["S1"]]

            def at(step, fn):
                later.setdefault(step, []).append(fn)

            def emit_s(J):
                i = state["si"]
                if i >= len(stiles):
                    return
                state["si"] += 1
                u, qt, h4, kb, mms = stiles[i]
                b = i % 2
                for m, (o, lt, rh, start, stop) in enumerate(mms):
                    p = add("pe", lambda e, o=o, lt=lt, rh=rh, start=start, stop=stop, b=b: e.matmul(
                        Sb[b][:, o[0]:o[1]], lt, rh, start=start, stop=stop, skip_group_check=not start),
                        f"{tag}_S", [sfree[b]] + (s_ready(u) if m == 0 else []))
                n = max(o[1] for o, *_ in mms)
                sfree[b] = add("dv", lambda e: e.tensor_reduce(mx[:, u, 4 * qt + h4, kb:kb + 1], Sb[b][:, 0:n], AX.X, ALU.max),
                               f"{tag}_mx", [p])
                last = i + 1 == len(stiles) or stiles[i + 1][0] != u
                if last:
                    nk = max(x[3] for x in stiles if x[0] == u) + 1
                    a = add("dv", lambda e: e.tensor_reduce(nm[:, u, :], mx[:, u, :, 0:nk], AX.X, ALU.max, negate=True),
                            f"{tag}_nm", [sfree[b]])
                    nv = nm[:, u, :]
                    rv = nr[:, u, :]
                    z = n3[:, u, :, :, :].rearrange("p q h s -> p (q h) s")
                    a = add("po", lambda e: e.tensor_copy(z[:, :, 0], nv), f"{tag}_n3", [a])
                    a = add("po", lambda e: e.tensor_tensor(rv, nv, z[:, :, 0], ALU.subtract), f"{tag}_n3", [a])
                    a = add("po", lambda e: e.tensor_copy(z[:, :, 1], rv), f"{tag}_n3", [a])
                    t_n3 = add("po", lambda e: e.tensor_tensor(z[:, :, 2], rv, z[:, :, 1], ALU.subtract), f"{tag}_n3", [a])

                    def turn():
                        Mh = Mb[:, :].bitcast(BF16)
                        for qt_ in range(4):
                            p = add("pe", lambda e, qt_=qt_: e.transpose(Mh[0:12, 128 * qt_:128 * qt_ + 128],
                                    n3[:, u, qt_, :, :].rearrange("p h s -> p (h s)"), idb[:, :]),
                                    f"{tag}_mT", [t_n3, free["M"], t_idb])
                        a = add("ac", lambda e: e.activation(nrow[:, u % 2, :], Mh[0:12, 0:CH], ACT.Copy), f"{tag}_nr",
                                [p, shift[u - 2] if u >= 2 else shift0[u % 2]])
                        free["M"] = a
                        for h4_ in range(4):
                            shift[u] = dma(shift_dst(u, h4_), nrow[3 * h4_:3 * h4_ + 3, u % 2, :], f"{tag}_sh{u}", [a])
                    at(J + 2, turn)

            shift0 = attention.shift_last
            afree = [free["A0"], free["A1"]]
            pv_tok = {}
            ex_tok = {}
            o_free = [free["O"]]

            def emit_st(j, pair):
                u, kt = steps[j]
                lo, mms = stmm(u, kt, pair)
                for m, (o, lt, rh, start, stop) in enumerate(mms):
                    p = add("pe", lambda e, o=o, lt=lt, rh=rh, start=start, stop=stop: e.matmul(
                        At[pair][:, o[0]:o[1]], lt, rh, start=start, stop=stop, skip_group_check=not start),
                        f"{tag}_T", [afree[pair], shift[u]] + (st_ready(u) if m == 0 else []))
                slot = (2 * j + pair) % 4
                ai = At[pair][:, :].rearrange("p (i n) -> p i n", i=2)[:, :, lo:CH]
                ao = PT[slot][:, :].rearrange("p (i n) -> p i n", i=2)[:, :, lo:CH]
                t = add("ac", lambda e: e.activation(ao, ai, ACT.Exp), f"{tag}_ex", [p, pv_tok.get((j - 2, pair))])
                afree[pair] = t
                ex_tok[(j, pair)] = t

            def emit_pv(j, pair):
                if j < 0:
                    return
                u, kt = steps[j]
                lo = width(u, kt)
                slot = (2 * j + pair) % 4
                for i in range(2):
                    g = 2 * pair + i
                    p = add("pe", lambda e, g=g, i=i: e.matmul(Ob[32 * g:32 * g + 32, lo:CH], vmm(u, kt, g),
                            PT[slot][:, CH * i + lo:CH * i + CH], start=(kt == 0), stop=True,
                            skip_group_check=(kt > 0), tile_position=(0, 32 * g)), f"{tag}_pv", [ex_tok[(j, pair)], o_free[0], d_ready(u)])
                pv_tok[(j, pair)] = p
                if kt == n_of[u] - 1 and pair == 1:
                    finish(u, j, p)

            def finish(u, j, p):
                c, quad = units[u]
                prev = os_tok[u % 2]
                o = add("ac", lambda e: e.activation(Os[:, u % 2, :], Ob[:, :], ACT.Copy), f"{tag}_os", [p, prev])
                o_free[0] = o

                def turn():
                    for qt in range(4):
                        p = add("pe", lambda e, qt=qt: e.transpose(Mb[:, 128 * qt:128 * qt + 128],
                                Os[:, u % 2, 128 * qt:128 * qt + 128], idf[:, :]), f"{tag}_oT", [o, free["M"]])
                    os_tok[u % 2] = p
                    Mq = Mb[:, :].rearrange("p (x w) -> p x w", w=32)
                    r = add("dv", lambda e: e.reciprocal(rl[:, u, :], Mq[:, :, dcols]), f"{tag}_rl", [p])
                    nq = 128 // (4 * dcols)
                    for qt in range(4):
                        w = add("dv", lambda e, qt=qt: e.tensor_tensor(
                            vw[:, c % 2, qt, 4 * dcols * quad:4 * dcols * quad + 4 * dcols].rearrange("p (g d) -> p g d", d=dcols),
                            Mq[:, 4 * qt:4 * qt + 4, 0:dcols],
                            rl[:, u, 4 * qt:4 * qt + 4].unsqueeze(2).to_broadcast([128, 4, dcols]), ALU.mult),
                            f"{tag}_vw", [r, vw_tok[c % 2]])
                    free["M"] = w
                    if quad == nq - 1:
                        def back():
                            for qt in range(4):
                                p = add("pe", lambda e, qt=qt: e.transpose(Mb[:, 128 * qt:128 * qt + 128],
                                        vw[:, c % 2, qt, :], idf[:, :]), f"{tag}_wT", [w, free["M"]])
                            vw_tok[c % 2] = p
                            a = add("ac", lambda e: e.activation(vwT[:, c % 2, :], Mb[:, :], ACT.Copy), f"{tag}_wc",
                                    [p, y_tok[c % 2]])
                            free["M"] = a
                            at(now[0] + 1, lambda: project(a))

                        def project(a):
                            for qt in range(4):
                                p = add("pe", lambda e, qt=qt: e.matmul(Mb[:, 128 * qt:128 * qt + 128],
                                        vwT[:, c % 2, 128 * qt:128 * qt + 128], wout[:, :], start=True, stop=True),
                                        f"{tag}_y", [a, t_wout])
                            y_tok[c % 2] = p
                            xv = xs[:, 4 * c:4 * c + 4, :]
                            x = add("dv", lambda e: e.tensor_tensor(xv, xv, Mb[:, :].rearrange("p (t n) -> p t n", t=4), ALU.add),
                                    f"{tag}_x", [p, x_ready])
                            free["M"] = x
                            x_done[c] = x
                        at(now[0] + 1, back)
                at(now[0] + 2, turn)

            os_tok, vw_tok, y_tok = attention.os_tok, attention.vw_tok, attention.y_tok
            now = [-2]

            def do_later():
                while True:
                    ks = [k for k in later if k <= now[0]]
                    if not ks:
                        break
                    for k in sorted(ks):
                        for fn in later.pop(k):
                            fn()

            cum = 0
            for J in range(len(steps) + 1):
                now[0] = J
                if J < len(steps):
                    u = steps[J][0]
                    nxt = n_of[u + 1] if u + 1 < nU else 0
                    target = min(4 * (J + nxt + 5), len(stiles))
                else:
                    target = len(stiles)
                k = max(0, target - state["si"])
                if J == 0:
                    first = len([1 for x in stiles if x[0] == 0])
                    for _ in range(first):
                        emit_s(-2)
                    do_later()
                    k = max(0, target - state["si"])
                    for _ in range(max(0, k - 4)):
                        emit_s(J)
                    do_later()
                    k = max(0, target - state["si"])
                do_later()
                parts = [k // 4 + (1 if i < k % 4 else 0) for i in range(4)]
                for i in range(4):
                    for _ in range(parts[i]):
                        emit_s(J)
                    if i % 2 == 0:
                        if J < len(steps):
                            emit_st(J, i // 2)
                    else:
                        emit_pv(J - 1, i // 2)
            while later:
                now[0] += 1
                do_later()
            free["S0"], free["S1"] = sfree
            free["A0"], free["A1"] = afree
            free["O"] = o_free[0]
            attention.shift_last = [shift[nU - 2], shift[nU - 1]] if nU % 2 == 0 else [shift[nU - 1], shift[nU - 2]]
            attention.last_pv = pv_tok[(len(steps) - 1, 1)]
            attention.last_ex = [afree[0], afree[1]]
            return x_done

        attention.shift_last = [None, None]
        attention.os_tok, attention.vw_tok, attention.y_tok = [None, None], [None, None], [None, None]

        units0 = [(c, q) for c in range(4) for q in range(4)]

        def s0(u, _):
            c, quad = units0[u]
            r = []
            for qt in range(4):
                for kb in range(4):
                    for h4 in range(4):
                        hd = 4 * quad + h4
                        ro, pr = 64 * (hd % 2), hd // 2
                        r.append((qt, h4, kb, [((0, CH), Qs[ro:ro + 48, pr, CH * c + 128 * qt:CH * c + 128 * qt + 128],
                                                Ks[ro:ro + 48, pr, CH * kb:CH * kb + CH], True, True)]))
            return r

        def st0(u, kt, pair):
            c, quad = units0[u]
            r = []
            for i in range(2):
                hd = 4 * quad + 2 * pair + i
                ro, pr = 64 * (hd % 2), hd // 2
                r.append(((CH * i, CH * i + CH), Ks[ro:ro + 51, pr, 128 * kt:128 * kt + 128],
                          Qs[ro:ro + 51, pr, CH * c:CH * c + CH], True, True))
            return 0, r

        def sh0(u, h4):
            c, quad = units0[u]
            hd = 4 * quad + h4
            ro = 64 * (hd % 2) + 48
            return Qs[ro:ro + 3, hd // 2, CH * c:CH * c + CH]

        xd0 = attention(0, units0, s0, st0, lambda u, kt, g: Va[:, kt, 4 * units0[u][1] + g, :],
                        lambda u, kt: 16 if kt is None else 0, 8, lambda u: t_v[3], sh0, woT, t_wo, t_xb,
                        lambda u: [t_k[3], t_k[2], t_k[1], t_k[0], t_q[units0[u][0]]],
                        lambda u: [t_k1, t_k[3], t_q[units0[u][0]]])
        pv0 = attention.last_pv

        mkd = [PT[0][:, 0:CH], PT[0][:, CH:], PT[1][:, 0:CH], PT[1][:, CH:]]
        ams = [PT[2][:, 0:CH], PT[2][:, CH:], PT[3][:, 0:CH], PT[3][:, CH:]]
        Gp, Up, Gs_, Us_ = A0, A1, A2, A3
        bt, bsg, hs = Os, qf, vwT[:, 0, :]
        F = {"mk": [pv0] * 4, "am": [pv0] * 4, "mask": [None] * 16, "bt": [None, None], "bsg": [None, None], "hs": None}
        gfree = {"G": [free["A0"]], "H": [free["A1"]]}
        xd1 = {}

        def mbs(n):
            return Ks[:, n // 4, CH * (n % 4):CH * (n % 4) + CH]

        def silu_mul(G, U, key, p, dst, dst_free, k):
            a = add("ac", lambda e: e.activation(bsg[:, k, :], G, ACT.Sigmoid), "ff_sg", [p, F["bsg"][k]])
            b = add("dv", lambda e: e.tensor_tensor(bt[:, k, :], G, bsg[:, k, :], ALU.mult), "ff_d", [a, F["bt"][k]])
            F["bsg"][k] = b
            d = add("dv", lambda e: e.tensor_tensor(dst, U, bt[:, k, :], ALU.mult), "ff_d", [b, dst_free])
            F["bt"][k] = d
            gfree[key] = [d]
            return d

        t_E = add("dv", lambda e: e.tensor_copy(E, idf[0:16, 0:16].unsqueeze(2).to_broadcast([16, 16, 128])), "ff_E", [t_id])
        hx = {}
        hx[0] = ln(0, 0, True, Sb[0][:, :], "S0", xd0[0], hts[0][0], "f0", xh_free=xp_last)
        def experts(c):
            h = hx[c][0]
            for j in range(4):
                p = add("pe", lambda e, c=c, j=j: e.matmul(Mb[:, 16 * j:16 * j + 16], hc(c, 128 * j, 128 * j + 128), rwT[:, :],
                                                           start=True, stop=True), "ff_lg", [h, free["M"], l1])
            a = add("dv", lambda e: e.tensor_copy(lg, Mb[:, 0:64].rearrange("p (t n) -> p t n", t=4)), "ff_r", [p])
            free["M"] = a
            a = add("dv", lambda e: e.tensor_reduce(lm[:, :], lg, AX.X, ALU.max), "ff_r", [a])
            sg = add("ac", lambda e: e.activation(sgm[:, :], lm[:, :], ACT.Sigmoid), "ff_sm", [a])
            a = add("dv", lambda e: e.tensor_tensor(eq, lg, lm[:, :].unsqueeze(2).to_broadcast([128, 4, 16]), ALU.is_equal), "ff_r", [a])
            a = add("dv", lambda e: e.tensor_tensor(wv_, eq, desc[:, :].unsqueeze(1).to_broadcast([128, 4, 16]), ALU.mult), "ff_r", [a])
            a = add("dv", lambda e: e.tensor_reduce(wm[:, :], wv_, AX.X, ALU.max), "ff_r", [a])
            a = add("dv", lambda e: e.tensor_tensor(oh, wv_, wm[:, :].unsqueeze(2).to_broadcast([128, 4, 16]), ALU.is_equal), "ff_r", [a])
            b = add("dv", lambda e: e.tensor_copy(ohb[:, :, :], oh), "ff_r", [a])
            b = add("dv", lambda e: e.tensor_tensor(soh, oh, sgm[:, :].unsqueeze(2).to_broadcast([128, 4, 16]), ALU.mult), "ff_r", [a, sg])

            sh_toks = []
            shb = []

            def shared_block(bl):
                key = "GH"[bl % 2]
                G, U = ((Gp, Up), (Gs_, Us_))[bl % 2]
                for W, O_ in ((sgT, G), (suT, U)):
                    p = add("pe", lambda e, W=W, O_=O_: e.matmul(O_, W[:, 128 * bl:128 * bl + 128], hc(c), start=True, stop=True),
                            "ff_sh", [h] + gfree[key])
                sh_toks.append((bl, silu_mul(G, U, key, p, ams[bl], F["am"][bl], bl % 2)))

            for bl in range(4):
                shared_block(bl)
                if bl == 1:
                    Mh = Mb[:, :].bitcast(BF16)
                    for j in range(4):
                        p = add("pe", lambda e, j=j: e.transpose(Mh[0:16, 128 * j:128 * j + 128], ohb[:, j, :], idb[:, :]), "ff_tr", [b, free["M"]])
                    a = add("dv", lambda e: e.tensor_copy(ohT, Mh[0:16, 0:CH]), "ff_o", [p])
                    for j in range(4):
                        p = add("pe", lambda e, j=j: e.transpose(Sb[1][0:16, 128 * j:128 * j + 128], soh[:, j, :], idf[:, :]), "ff_tr", [b, free["S1"]])
                    a2 = add("dv", lambda e: e.tensor_copy(sT, Sb[1][0:16, :]), "ff_o", [p])
                    p = add("pe", lambda e: e.matmul(Mb[:, :], onesf[0:16, :], sT, start=True, stop=True), "ff_sb", [a, a2, t_one])
                    t_hs = add("dv", lambda e, c=c: e.tensor_tensor(hs, hc(c), Mb[:, :], ALU.mult), "ff_o", [p, h])
                    free["M"] = t_hs
                    free["S1"] = a2
            first_y = [True]

            def down(am, w, tok, sig="ff_y"):
                for j in range(4):
                    p = add("pe", lambda e, j=j, s=first_y[0] and j == 0: e.matmul(Ob[:, 128 * j:128 * j + 128], am[:, 128 * j:128 * j + 128], w,
                                                     start=s, stop=True, skip_group_check=True), sig, [tok, free["O"], t_dn])
                first_y[0] = False
                return p
            exp_banks = [("S1", Sb[1]), ("M", Mb)]
            mtoks = {}

            def mask(n):
                key, bank = exp_banks[n % 2]
                p = add("pe", lambda e: e.matmul(bank[:, :], E[:, n, :], ohT, start=True, stop=True), "ff_mb", [free[key], a, t_E])
                cpy = add("ac", lambda e: e.activation(mbs(n), bank[:, :], ACT.Copy), "ff_mc", [p, F["mask"][n], pv0])
                k = n % 4
                m_ = add("dv", lambda e: e.tensor_tensor(mkd[k], hs, bank[:, :], ALU.mult), "ff_mk", [cpy, t_hs, F["mk"][k]])
                free[key] = m_
                mtoks[n] = (m_, cpy)

            mask(0)
            mask(1)
            for bl, tok in sh_toks:
                F["am"][bl] = down(ams[bl], sdT[:, bl, :], tok)
                if bl < 2:
                    mask(2 + bl)
            for n in range(16):
                for W, O_ in ((0, Gp), (128, Up)):
                    p = add("pe", lambda e, W=W, O_=O_, n=n: e.matmul(O_, gu[:, n, W:W + 128], mkd[n % 4], start=(n == 0), stop=(n == 15)),
                            "ff_e", [mtoks[n][0]] + gfree["G"] + gfree["H"])
                F["mk"][n % 4] = p
                if n + 4 < 16:
                    mask(n + 4)
            d = silu_mul(Gp, Up, "G", p, hs, None, 0)
            if c < 3:
                hx[c + 1] = ln(c + 1, 0, True, Sb[0][:, :], "S0", xd0[c + 1], hts[c + 1][0], f"f{c+1}", xh_free=xp_last)
            for n in range(16):
                k = n % 4
                eng = "po" if n % 3 == 1 else "dv"
                m_ = add(eng, lambda e, n=n, k=k: e.tensor_tensor(ams[k], hs, mbs(n), ALU.mult), "ff_am_" + eng, [d, mtoks[n][1], F["am"][k]])
                F["mask"][n] = m_
                F["am"][k] = down(ams[k], dn[:, n, :], m_)
            xv = xs[:, 4 * c:4 * c + 4, :]
            x = add("dv", lambda e, xv=xv: e.tensor_tensor(xv, xv, Ob[:, :].rearrange("p (t n) -> p t n", t=4), ALU.add),
                    "ff_x", [F["am"][3]])
            free["O"] = x
            xd1[c] = x

        for c in range(4):
            experts(c)
        free["A0"] = free["A1"] = gfree["G"][0]
        ffn_h = hx

        t_q1, t_kk, t_v1s, h1 = [], [], [], []
        for c in range(4):
            h, xp = ln(c, 1, False, Mb[:, :], "M", xd1[c], F["am"][3], f"g{c}", xh_free=ffn_h[3][1])
            h1.append((h, xp))
            cols = slice(CH * c, CH * c + CH)
            p = add("pe", lambda e, c=c: e.matmul(Sb[1][0:16, :], wk1[:, :], hc(c), start=True, stop=True), "pe_p1", [h, free["S1"]])
            tw = split(Sb[1], "S1", p, 16, None, 1.0, dk1[:, :, cols])
            for j in range(6):
                tl = dma(Ks[16 * j:16 * j + 16, 7, cols], dk1[KP[j], :, cols], f"sl2{c}", [tw, pv0])
            t_kk.append(tl)
            p = add("pe", lambda e, c=c: e.matmul(Sb[0][:, :], wq1[:, :], hc(c), start=True, stop=True), "pe_p1", [free["S0"]])
            tw = split(Sb[0], "S0", p, 128, None, 128.0 ** -0.5, dq1[:, :, cols])
            for j in range(6):
                tl = dma(Qs[16 * j:16 * j + 16, :, cols], dq1[QP[j]].rearrange("(q d) n -> d q n", d=16)[:, :, cols], f"sl3{c}", [tw, pv0])
            t_q1.append(tl)
            for j in range(4):
                p = add("pe", lambda e, c=c, j=j: e.matmul(Ob[:, 128 * j:128 * j + 16], hc(c, 128 * j, 128 * j + 128), wv1[:, :],
                                                           start=True, stop=True), "pe_p1", [free["O"]])
            t = add("dv", lambda e, c=c: e.tensor_copy(V1[:, 4 * c:4 * c + 4, 0:16], Ob[:, :].rearrange("p (t n) -> p t n", t=4)[:, :, 0:16]),
                    "dv_v", [p, t_v1])
            free["O"] = t
            t_v1s.append(t)
        t_k1b = dma(Ks[96:99, 7, :], Ks[48:51, 6, :], "ld_ones1", [pv0, t_k1])
        for c in range(4):
            t_xb1 = add("po", lambda e, c=c: e.tensor_tensor(xs[:, 4 * c:4 * c + 4, :], xs[:, 4 * c:4 * c + 4, :],
                        bpB[:, :].unsqueeze(1).to_broadcast([128, 4, 128]), ALU.add), "po_xb", [h1[c][1]])

        units1 = [(c, q) for c in range(4) for q in range(2)]

        def s1(u, _):
            c, quad = units1[u]
            r = []
            for qt in range(4):
                for kb in range(c + 1):
                    for h4 in range(4):
                        qap = Qs[0:96, 4 * quad + h4, CH * c + 128 * qt:CH * c + 128 * qt + 128]
                        n = CH if kb < c else 128 * (qt + 1)
                        m = [((0, n), qap, Ks[0:96, 7, CH * kb:CH * kb + n], True, True)]
                        if kb == c:
                            m.append(((n - 128, n), idb[:, :], mq[:, :], False, True))
                        r.append((qt, h4, kb, m))
            return r

        def st1(u, kt, pair):
            c, quad = units1[u]
            lo = width1(u, kt)
            diag = kt >= 4 * c
            r = []
            for i in range(2):
                hd = 4 * quad + 2 * pair + i
                r.append(((CH * i + lo, CH * i + CH), Ks[0:99, 7, 128 * kt:128 * kt + 128],
                          Qs[0:99, hd, CH * c + lo:CH * c + CH], True, True))
                if diag:
                    r.append(((CH * i + lo, CH * i + lo + 128), idb[:, :], mk[:, :], False, True))
            return lo, r

        def width1(u, kt):
            c = units1[u][0]
            if kt is None:
                return 4 * (c + 1)
            return max(0, 128 * (kt - 4 * c))

        xd2 = attention(1, units1, s1, st1, lambda u, kt, g: V1[:, kt, :], width1, 16, lambda u: t_v1s[3],
                        lambda u, h4: Qs[96:99, 4 * units1[u][1] + h4, CH * units1[u][0]:CH * units1[u][0] + CH],
                        wp1, t_wp, t_xb1,
                        lambda u: t_kk[0:units1[u][0] + 1] + t_q1[0:units1[u][0] + 1],
                        lambda u: [t_k1b])

        pv1 = attention.last_pv
        hx = {}
        t_out = None
        for c in range(4):
            hx[c] = ln(c, 1, True, Sb[c % 2][:, :], f"S{c % 2}", xd2[c], h1[c][0], f"k{c}", xh_free=h1[3][1])
        tr_free = [pv1, pv1]
        for c in range(4):
            s = c % 2
            hp = hT[:, CH * c:CH * c + CH]
            h = hx[c][0]
            xr, xk = PT[s][:, 0:CH], PT[s][:, CH:]
            kr, ka = PT[2 + s][:, 0:CH], PT[2 + s][:, CH:]
            hb = hx[max(c - 1, 0)][0]
            add("dv", lambda e, c=c, xr=xr: e.tensor_scalar(xr, hc(c), mur[:, 0:1], None, ALU.mult), "cm_d", [h, hb, tr_free[s], t_om])
            d = add("dv", lambda e, c=c, xk=xk: e.tensor_scalar(xk, hc(c), muk[:, 0:1], None, ALU.mult), "cm_d")
            add("dv", lambda e, xk=xk, hp=hp: e.scalar_tensor_tensor(xk, hp, omk[:, 0:1], xk, ALU.mult, ALU.add), "cm_d", [d])
            d = add("dv", lambda e, xr=xr, hp=hp: e.scalar_tensor_tensor(xr, hp, omr[:, 0:1], xr, ALU.mult, ALU.add), "cm_d")
            pk = add("pe", lambda e, s=s, xk=xk: e.matmul(At[s][:, 0:CH], wkk[:, :], xk, start=True, stop=True), "cm_p", [d, free[f"A{s}"]])
            for j in range(4):
                pr = add("pe", lambda e, s=s, j=j, xr=xr: e.matmul(At[s][:, CH + 128 * j:CH + 128 * j + 128], xr[:, 128 * j:128 * j + 128], wr[:, :],
                                                            start=True, stop=True), "cm_p")
            a = add("dv", lambda e, s=s, kr=kr: e.tensor_scalar(kr, At[s][:, 0:CH], 0.0, None, ALU.max), "cm_d", [pk])
            a = add("dv", lambda e, kr=kr, ka=ka: e.tensor_tensor(ka, kr, kr, ALU.mult), "cm_d", [a])
            sg = add("ac", lambda e, s=s: e.activation(bsg[:, s, :], At[s][:, CH:2 * CH], ACT.Sigmoid), "cm_a", [pr, F["bsg"][s]])
            free[f"A{s}"] = sg
            bank, key = ((Ob, "O"), (Mb, "M"))[s]
            for j in range(4):
                p = add("pe", lambda e, j=j, bank=bank, ka=ka: e.matmul(bank[:, 128 * j:128 * j + 128], ka[:, 128 * j:128 * j + 128], wvv[:, :],
                                                                start=True, stop=True), "cm_p", [a, free[key], t_wvv])
            tr_free[s] = p
            a = add("dv", lambda e, s=s, bank=bank: e.tensor_tensor(bt[:, s, :], bsg[:, s, :], bank[:, :], ALU.mult), "cm_d", [p, sg])
            F["bsg"][s] = a
            free[key] = a
            xv = xs[:, 4 * c:4 * c + 4, :]
            x = add("dv", lambda e, s=s, xv=xv: e.tensor_tensor(xv, xv, bt[:, s, :].rearrange("p (t n) -> p t n", t=4), ALU.add), "cm_d", [a, hx[c][1]])
            t_out = dma(out.rearrange("a (t p) n -> p (a t) n", p=128)[:, 4 * c:4 * c + 4, :], xv, "st_out", [x])
        queues["sp"].append((None, None, 0, [t_out]))

        block = ctx.enter_context(nc.Block())

        @block.sync
        def _(e):
            tail = queues["sp"].pop()
            run("sp", e)
            for s, v in tail[3]:
                e.wait_ge(sems[s], v)

        @block.tensor
        def _(e):
            run("pe", e)

        @block.vector
        def _(e):
            run("dv", e)

        @block.scalar
        def _(e):
            run("ac", e)

        @block.gpsimd
        def _(e):
            run("po", e)


_TURNED = ('L0_attn_Wq', 'L0_attn_Wk', 'L0_attn_Wv', 'L0_attn_Wo', 'L0_ffn_router_w', 'L0_ffn_shared_gate_w',
           'L0_ffn_shared_up_w', 'L0_ffn_shared_down_w', 'L1_ffn_W_r', 'L1_ffn_W_k', 'L1_ffn_W_v')


def kernel(**inputs):
    import numpy as _np
    import concourse.bacc as _bacc
    from concourse import mybir as _mybir
    from concourse.bass_utils import run_bass_kernel_spmd as _run

    nc = _bacc.Bacc("TRN2", target_bir_lowering=False, num_devices=1)
    arrays, args = {}, {}
    for name in inputs:
        a = _np.asarray(inputs[name])
        a = _np.ascontiguousarray(a.T if name in _TURNED else a)
        arrays[f"in_{name}"] = a
        args[name] = nc.dram_tensor(f"in_{name}", a.shape, _mybir.dt.from_np(a.dtype), kind="ExternalInput").ap()
    o = nc.dram_tensor("out_0", (1, 2048, 128), _mybir.dt.float32, kind="ExternalOutput").ap()
    adaln_two_layers(nc, args, o)
    r = _run(nc, [arrays], core_ids=[0])
    return r.results[0]["out_0"]
```

```python
import concourse.bass as bass
from concourse import mybir
from contextlib import ExitStack

F32 = mybir.dt.float32
BF16 = mybir.dt.bfloat16
ALU = mybir.AluOpType
ACT = mybir.ActivationFunctionType
AX = mybir.AxisListType

S = 2048
NC_ = 4
CH = 512
EPS = 1e-5
NEG = -1e30


def adaln_two_layers(nc, A, out):
    ctx = ExitStack()
    with ctx:
        def sb(name, shape, dt=F32):
            return ctx.enter_context(nc.sbuf_tensor(name, shape, dt))

        def pb(name, shape):
            return ctx.enter_context(nc.psum_tensor(name, shape, F32))

        queues = {"pe": [], "dv": [], "ac": [], "po": [], "sp": []}
        sems, counts = {}, {}

        def sem(name):
            if name not in sems:
                sems[name] = ctx.enter_context(nc.semaphore(name))
                counts[name] = 0
            return sems[name]

        def add(eng, fn, sig=None, after=(), by=1):
            tok = None
            if sig is not None:
                sem(sig)
                counts[sig] += by
                tok = (sig, counts[sig])
            queues[eng].append((fn, sig, by, [t for t in after if t is not None]))
            return tok

        def dma(dst, src, sig, after=(), eng="sp"):
            return add(eng, lambda e: e.dma_start(dst, src), sig, after, by=16)

        def run(name, e):
            seen = {}
            for fn, sig, by, after in queues[name]:
                for s, v in after:
                    if seen.get(s, 0) < v:
                        e.wait_ge(sems[s], v)
                        seen[s] = v
                ins = fn(e)
                if sig is not None:
                    ins.then_inc(sems[sig], by)

        Qs = sb("Qs", [128, 16, 2 * CH], BF16)
        Q1 = Qs[:, :, :].rearrange("p h n -> p (h n)").rearrange("p (h n) -> p h n", h=8)
        Ks = sb("Ks", [128, 8, S], BF16)
        Va = sb("Va", [128, 16, 16, 32])
        V1 = sb("V1", [128, 16, 32])
        xs = sb("xs", [128, 16, 128])
        hT = sb("hT", [128, 1 + S])
        xh = sb("xh", [128, 8, 128])
        PT = [sb(f"PT{i}", [128, 1024]) for i in range(4)]
        qf = sb("qf", [128, 2, CH])
        q3 = sb("q3", [128, 2, 3, CH], BF16)
        st = sb("st", [128, 16, 6])
        mv = sb("mv", [128, 16, 2])
        ve = sb("ve", [128, 16])
        rs = sb("rs", [128, 16])
        mh = sb("mh", [128, 4])
        Os = sb("Os", [128, 2, CH])
        rl = sb("rl", [128, 16, 16])
        vw = sb("vw", [128, 2, 4, 128])
        vwT = sb("vwT", [128, 2, CH])
        mxr = sb("mx", [128, 1024])
        mx = mxr[:, :].rearrange("p (u q k) -> p u q k", u=16, k=4)
        nm = sb("nm", [128, 16, 16])
        nr = sb("nr", [128, 16, 16])
        n3 = sb("n3", [128, 16, 4, 4, 3], BF16)
        nrow = sb("nrow", [12, 2, CH], BF16)
        idf = sb("idf", [128, 128])
        idb = sb("idb", [128, 128], BF16)
        mq = sb("mq", [128, 128], BF16)
        mk = sb("mk", [128, 128], BF16)
        E = mxr[0:16, :].bitcast(BF16).rearrange("p (n m) -> p n m", n=16)
        onesf = sb("onesf", [128, 128])
        wqT, wkT, wvT, woT = (sb(n, [128, 128]) for n in ("wqT", "wkT", "wvT", "woT"))
        bq, bk, bqs = (sb(n, [128, 1]) for n in ("bq", "bk", "bqs"))
        bvB, boB, bpB = (sb(n, [128, 128]) for n in ("bvB", "boB", "bpB"))
        rwT = sb("rwT", [128, 16])
        gu = sb("gu", [128, 16, 256])
        dn = sb("dn", [128, 16, 128])
        sgT, suT = sb("sgT", [128, CH]), sb("suT", [128, CH])
        sdT = sb("sdT", [128, 4, 128])
        wk1, wv1 = sb("wk1", [128, 16]), sb("wv1", [128, 16])
        wq1 = sb("wq1", [128, 128])
        wp1 = sb("wp1", [128, 128])
        wr, wkk, wvv = (sb(n, [128, 128]) for n in ("wr", "wkk", "wvv"))
        mur, muk, omr, omk = (sb(n, [128, 1]) for n in ("mur", "muk", "omr", "omk"))
        desc = sb("desc", [128, 16])
        mods = []
        cc = sb("cc", [128, 2])
        csg = sb("csg", [128, 2])
        cs = sb("cs", [128, 2])
        cb = PT[1][:, 768:1024].rearrange("p (i n) -> p i n", i=2)
        mc = sb("mc", [128, 2, 4])
        gB = sb("gB", [128, 4, 128])
        gt = PT[2][:, :].rearrange("p (a g n) -> p a g n", a=2, g=4)
        lg, eq, wv_, oh = (nm[:, 4 * i:4 * i + 4, :] for i in range(4))
        soh = nr[:, 0:4, :]
        ohb = sb("ohb", [128, 4, 16], BF16)
        lm, wm, sgm = (sb(n, [128, 4]) for n in ("lm", "wm", "sgm"))
        sT = vw[0:16, 0, :, :].rearrange("p t n -> p (t n)")
        ohT = vw[0:16, 1, :, :].rearrange("p t n -> p (t n)").bitcast(BF16)[:, 0:CH]

        At = [pb("At0", [128, 1024]), pb("At1", [128, 1024])]
        Sb = [pb("Sb0", [128, CH]), pb("Sb1", [128, CH])]
        Ob = pb("Ob", [128, CH])
        Mb = pb("Mb", [128, CH])
        A0, A1, A2, A3 = (At[i // 2][:, CH * (i % 2):CH * (i % 2) + CH] for i in range(4))


        scratch = {n: nc.dram_tensor(f"rows_{n}", [6, 16 if n == "k1" else 128, S], BF16).ap() for n in ("q", "k", "q1", "k1")}

        xd = A["L0_attn_x"].rearrange("a (t p) n -> p (a t) n", p=128)
        lx = [dma(xs[:, 4 * c:4 * c + 4, :], xd[:, 4 * c:4 * c + 4, :], f"ld_x{c}") for c in range(4)]
        dma(cc[:, 0:1], A["L0_c"].rearrange("a n -> n a"), "ld_c", eng="ac")
        lc = dma(cc[:, 1:2], A["L1_c"].rearrange("a n -> n a"), "ld_c", eng="ac")
        wm_sb = [PT[0], PT[1]]
        lw = None
        for i in range(2):
            lw = dma(wm_sb[i][:, 0:768], A[f"L{i}_wmod"], "ld_wm", eng="ac")
        def col(v):
            return v.rearrange("(n a) -> n a", a=1)
        for dst, src in ((wqT, A["L0_attn_Wq"]), (wkT, A["L0_attn_Wk"]), (wvT, A["L0_attn_Wv"])):
            l0 = dma(dst[:, :], src, "ld_w0")
        for dst, src in ((bq, "L0_attn_bq"), (bk, "L0_attn_bk")):
            l0 = dma(dst[:, :], col(A[src]), "ld_w0")
        l0 = dma(bvB[:, :], A["L0_attn_bv"].partition_broadcast(128), "ld_w0")
        for dst, src in ((woT[:, :], A["L0_attn_Wo"]),
                         (boB[:, :], A["L0_attn_bo"].partition_broadcast(128)),
                         (bpB[:, :], A["L1_attn_bp"].partition_broadcast(128)),
                         (rwT[:, :], A["L0_ffn_router_w"]),
                         (gu[:, :, :], A["L0_ffn_gate_up_proj"].rearrange("n h f -> h n f")),
                         (dn[:, :, :], A["L0_ffn_down_proj"].rearrange("n f h -> f n h")),
                         (sgT[:, :], A["L0_ffn_shared_gate_w"]), (suT[:, :], A["L0_ffn_shared_up_w"]),
                         (sdT[:, :, :], A["L0_ffn_shared_down_w"].rearrange("(b f) h -> f b h", f=128)),
                         (wk1[:, :], A["L1_attn_Wk"]), (wv1[:, :], A["L1_attn_Wv"]),
                         (wq1[:, :], A["L1_attn_Wq"].rearrange("c d q -> c (d q)")),
                         (wp1[:, :], A["L1_attn_Wp"]),
                         (wr[:, :], A["L1_ffn_W_r"]), (wkk[:, :], A["L1_ffn_W_k"]), (wvv[:, :], A["L1_ffn_W_v"]),
                         (mur[:, :], col(A["L1_ffn_mu_r"])), (muk[:, :], col(A["L1_ffn_mu_k"]))):
            l1 = dma(dst, src, "ld_w1")

        add("po", lambda e: e.memset(idf[:, :], 0.0), "c0")
        add("po", lambda e: e.memset(mq[:, :], 0.0), "c0")
        c0 = add("po", lambda e: e.memset(mk[:, :], 0.0), "c0")
        t_id = add("po", lambda e: e.affine_select(out=idf[:, :], in_=idf[:, :], compare_op=ALU.not_equal, fill=1.0,
                                                   base=0, pattern=[[-1, 128]], channel_multiplier=1), "c1", [c0])
        t_rs0 = None
        c1 = add("po", lambda e: e.affine_select(out=mq[:, :], in_=mq[:, :], compare_op=ALU.is_ge, fill=NEG,
                                                 base=0, pattern=[[-1, 128]], channel_multiplier=1), "c1")
        c1 = add("po", lambda e: e.affine_select(out=mk[:, :], in_=mk[:, :], compare_op=ALU.is_ge, fill=NEG,
                                                 base=0, pattern=[[1, 128]], channel_multiplier=-1), "c1")
        t_idb = add("po", lambda e: e.tensor_copy(idb[:, :], idf[:, :]), "c1", [t_id])
        add("po", lambda e: e.memset(mh[:, :], -0.5), "c1")
        t_one = add("po", lambda e: e.memset(hT[:, 0:1], 0.0), "c1")
        add("dv", lambda e: e.memset(onesf[:, :], 1.0), "c2")
        t_qz = add("po", lambda e: e.memset(Qs[:, :, :].bitcast(F32), 0.0), "c4")
        t_va = add("po", lambda e: e.memset(Va[:, :, :, :], 1.0), "c4")
        t_v1 = add("dv", lambda e: e.memset(V1[:, :, :], 1.0), "c2")
        for n in range(16):
            c2 = add("dv", lambda e, n=n: e.memset(desc[:, n:n + 1], float(16 - n)), "c2")

        t = add("ac", lambda e: e.activation(csg[:, :], cc[:, :], ACT.Sigmoid), "ac_set", [lc])
        t = add("dv", lambda e: e.tensor_tensor(cs[:, :], cc[:, :], csg[:, :], ALU.mult), "dv_set", [t, lc])
        for i in range(2):
            tcb = add("dv", lambda e, i=i: e.tensor_scalar(cb[:, i, :], onesf[:, :], cs[:, i:i + 1], None, ALU.mult),
                      "dv_set", [t, c2])
        for i in range(2):
            for k, j in enumerate((0, 1, 3, 4)):
                tm = add("pe", lambda e, i=i, j=j, k=k: e.matmul(Ob[:, 4 * i + k:4 * i + k + 1],
                         wm_sb[i][:, 128 * j:128 * j + 128], cs[:, i:i + 1], start=True, stop=True),
                         "pe_set", [lw, tcb])
        tmc = add("dv", lambda e: e.tensor_copy(mc[:, :, :], Ob[:, 0:8].rearrange("p (i k) -> p i k", i=2)), "dv_set", [tm])
        tmc = add("dv", lambda e: e.tensor_scalar(mc[:, :, 1:4:2], mc[:, :, 1:4:2], 1.0, None, ALU.add), "dv_set", [tmc])
        for i in range(2):
            for k, j in enumerate((2, 5)):
                g = 2 * i + k
                tm = add("pe", lambda e, i=i, j=j, g=g: e.matmul(Mb[:, 128 * g:128 * g + 128],
                         cb[:, i, :], wm_sb[i][:, 128 * j:128 * j + 128], start=True, stop=True), "pe_set")
        Mv = Mb[:, :].rearrange("p (g n) -> p g n", g=4)
        t1 = add("dv", lambda e: e.tensor_scalar(gt[:, 0, :, :], Mv, 0.0, 2.0, ALU.is_ge, ALU.mult), "dv_set", [tm])
        gf = gB[:, :, :].rearrange("p g n -> p (g n)")
        t2 = add("dv", lambda e: e.tensor_copy(gf, Mb[:, :]), "dv_set")
        free = {"M": t2, "O": tmc, "S0": None, "S1": None, "A0": None, "A1": None}
        t2 = add("dv", lambda e: e.scalar_tensor_tensor(PT[2][:, CH:], gf, -1.0, gf, ALU.mult, ALU.max), "dv_set", [t2])
        t2 = add("dv", lambda e: e.tensor_scalar(PT[2][:, CH:], PT[2][:, CH:], 0.25, None, ALU.max), "dv_set", [t2])
        tg = add("dv", lambda e: e.scalar_tensor_tensor(gB[:, :, :].rearrange("p g n -> p (g n)"), PT[2][:, 0:CH], -1.0,
                                                        PT[2][:, CH:], ALU.add, ALU.mult), "dv_set", [t2])
        tbq = add("dv", lambda e: e.tensor_scalar(bqs[:, :], bq[:, :], 8.0 ** -0.5, None, ALU.mult), "dv_set", [l0])
        def scale_w(w, g):
            return add("po", lambda e: e.tensor_tensor(w[:, :], w[:, :], gB[:, g, :], ALU.mult), "po_set", [tg, l1])
        t_wo = scale_w(woT, 0)
        scale_w(boB, 0)
        scale_w(bpB, 2)
        t_wp = scale_w(wp1, 2)
        t_wvv = scale_w(wvv, 3)
        add("po", lambda e: e.tensor_tensor(dn[:, :, :], dn[:, :, :], gB[:, 1, :].unsqueeze(1).to_broadcast([128, 16, 128]), ALU.mult), "po_set")
        t_dn = add("po", lambda e: e.tensor_tensor(sdT[:, :, :], sdT[:, :, :], gB[:, 1, :].unsqueeze(1).to_broadcast([128, 4, 128]), ALU.mult), "po_set")
        add("dv", lambda e: e.tensor_scalar(omr[:, :], mur[:, :], -1.0, 1.0, ALU.mult, ALU.add), "dv_om", [l1])
        t_om = add("dv", lambda e: e.tensor_scalar(omk[:, :], muk[:, :], -1.0, 1.0, ALU.mult, ALU.add), "dv_om")

        xh_tok = [None, None]

        def ln(c, layer, second, bank, bkey, x_ready, hT_free):
            xh_free = xh_tok[c % 2]
            k = 2 if second else 0
            for t_ in range(4 * c, 4 * c + 4):
                a = add("dv", lambda e, t_=t_: e.bn_stats(st[:, t_, :], xs[:, t_, :]), "dv_ln", [x_ready])
            for t_ in range(4 * c, 4 * c + 4):
                a = add("dv", lambda e, t_=t_: e.bn_aggr(mv[:, t_, :], st[:, t_, :]), "dv_ln", [a])
            cs_ = slice(4 * c, 4 * c + 4)
            b = add("po", lambda e: e.tensor_scalar(ve[:, cs_], mv[:, cs_, 1], EPS, None, ALU.add), "po_ln", [a])
            b = add("po", lambda e: e.tensor_tensor(rs[:, cs_], ve[:, cs_], mh[:, :], ALU.pow), "po_ln", [b, t_one])
            for t_ in range(4 * c, 4 * c + 4):
                d = add("dv", lambda e, t_=t_: e.tensor_scalar(xh[:, t_ % 8, :], xs[:, t_, :], mv[:, t_, 0:1], rs[:, t_:t_ + 1],
                                                               ALU.subtract, ALU.mult), "dv_xh", [b, xh_free])
            for j in range(4):
                p = add("pe", lambda e, j=j: e.transpose(bank[:, 128 * j:128 * j + 128], xh[:, (4 * c + j) % 8, :], idf[:, :]),
                        "pe_ln", [d, free[bkey], t_id])
            f = add("ac", lambda e: e.activation(hT[:, 1 + CH * c:1 + CH * c + CH], bank, ACT.Identity,
                                                 bias=mc[:, layer, k:k + 1], scale=mc[:, layer, k + 1:k + 2]),
                    "ac_h", [p, hT_free, tmc])
            free[bkey] = f
            xh_tok[c % 2] = p
            return f, p

        def hc(c, a=0, b=CH):
            return hT[:, 1 + CH * c + a:1 + CH * c + b]

        split_state = {"n": 0, "wr": [[], []]}

        def split(bank, bkey, ready, rows, bias, scale, place):
            n = split_state["n"]
            split_state["n"] += 1
            s = n % 2
            prev = split_state["wr"][s]
            f = qf[0:rows, s, :]
            if bias is None:
                a = add("ac", lambda e: e.activation(f, bank[0:rows, :], ACT.Copy, scale=scale), "ac_sp", [ready] + prev)
            else:
                a = add("ac", lambda e: e.activation(f, bank[0:rows, :], ACT.Identity, bias=bias, scale=scale), "ac_sp",
                        [ready, tbq] + prev)
            free[bkey] = a
            p = [q3[0:rows, s, i, :] for i in range(3)]
            b = add("ac", lambda e: e.activation(p[0], f, ACT.Copy), "ac_sp", [a])
            r = add("po", lambda e: e.tensor_tensor(f, f, p[0], ALU.subtract), "po_sp", [b])
            d = add("dv", lambda e: e.tensor_copy(p[1], f), "dv_sp", [r])
            g = add("po", lambda e: e.tensor_tensor(p[2], f, p[1], ALU.subtract), "po_sp", [d])
            split_state["wr"][s] = place(q3[0:rows, s, :, :], g)
            return split_state["wr"][s]

        RUNS = {"q": ((0, 3, 0), (3, 2, 1), (5, 1, 2)), "k": ((0, 3, 0), (3, 2, 0), (5, 1, 0))}

        def store_rows(kind, scr, parts, sig, tok):
            rows, _, n = parts.shape
            for j, k, p0 in RUNS[kind]:
                src = parts[:, p0:p0 + k, :] if kind == "k" else parts[:, p0:p0 + 1, :].to_broadcast([rows, k, n])
                t = dma(scr[j:j + k].rearrange("s p n -> p s n"), src, sig, [tok])
            return t

        t_q, t_k, t_v, hts = [], [], [], []

        def slab0(which, c, parts, tok):
            cols = slice(CH * c, CH * c + CH) if which == "k" else slice(CH * (c % 2), CH * (c % 2) + CH)
            scr = scratch[which][:, :, CH * c:CH * c + CH]
            tw = store_rows(which, scr, parts, f"sw{which}{c}", tok)
            for par in range(2):
                slab = Ks[48 * par:48 * par + 48, :, cols] if which == "k" else Qs[48 * par:48 * par + 48, par:16:2, cols]
                done = dma(slab, scr.rearrange("j (d two h) n -> two (j d) h n", two=2, h=8)[par], f"sl{which}{c}",
                           [tw] + ([t_qz] + q_free.get(c, []) if which == "q" else []))
            return [tw, done]

        q_free = {}

        def project_k(c):
            p = add("pe", lambda e: e.matmul(Sb[1][:, :], wkT[:, :], hc(c), start=True, stop=True), "pe_pr", [hts[c][0], free["S1"], l0])
            t_k.append(split(Sb[1], "S1", p, 128, bk[:, :], 1.0, lambda parts, g: slab0("k", c, parts, g))[1])

        def project_q(c, bank=Mb, key="M"):
            p = add("pe", lambda e: e.matmul(bank[:, :], wqT[:, :], hc(c), start=True, stop=True), "pe_pr", [hts[c][0], free[key], l0])
            t_q.append(split(bank, key, p, 128, bqs[:, :], 8.0 ** -0.5, lambda parts, g: slab0("q", c, parts, g))[1])

        def project_v(c):
            for j in range(4):
                p = add("pe", lambda e, j=j: e.matmul(Ob[:, 128 * j:128 * j + 128], hc(c, 128 * j, 128 * j + 128), wvT[:, :],
                                                      start=True, stop=True), "pe_pr", [free["O"], hts[c][0]])
            for j in range(4):
                t = add("dv", lambda e, j=j: e.tensor_tensor(
                    Va[:, 4 * c + j, :, 0:8], Ob[:, 128 * j:128 * j + 128].rearrange("p (h d) -> p h d", d=8),
                    bvB[:, :].rearrange("p (h d) -> p h d", d=8), ALU.add), "dv_v", [p, t_va, l0])
            free["O"] = t
            t_v.append(t)

        def setup0(c):
            hts.append(ln(c, 0, False, At[c % 2][:, 0:CH], f"A{c % 2}", lx[c], None))
            project_k(c)
            if c == 0:
                project_q(0, Sb[0], "S0")
            project_v(c)

        def output_bias0(c):
            return add("po", lambda e: e.tensor_tensor(xs[:, 4 * c:4 * c + 4, :], xs[:, 4 * c:4 * c + 4, :],
                       boB[:, :].unsqueeze(1).to_broadcast([128, 4, 128]), ALU.add), "po_xb", [hts[c][1], t_dn])

        def attention(L, units, smm, stmm, vmm, width, dcols, d_ready, shift_dst, wout, t_wout, x_ready, s_ready, st_ready,
                      before=(), hooks=(), on_chunk=None):
            nU = len(units)
            steps = [(u, kt) for u in range(nU) for kt in range(width(u, None))]
            stiles = []
            for u in range(nU):
                stiles += [(u,) + x for x in smm(u, None)]
            n_of = [width(u, None) for u in range(nU)]
            tag = f"L{L}"
            state = {"si": 0}
            later = {}
            shift = [None] * nU
            x_done = {}

            def at(step, fn):
                later.setdefault(step, []).append(fn)

            def emit_s(J):
                i = state["si"]
                if i >= len(stiles):
                    return
                state["si"] += 1
                u, qt, h4, kb, mms = stiles[i]
                b = i % 2
                for m, (o, lt, rh, start, stop) in enumerate(mms):
                    p = add("pe", lambda e, o=o, lt=lt, rh=rh, start=start, stop=stop, b=b: e.matmul(
                        Sb[b][:, o[0]:o[1]], lt, rh, start=start, stop=stop, skip_group_check=not start),
                        f"{tag}_S", [free[f"S{b}"]] + (s_ready(u, kb) if m == 0 else []))
                n = max(o[1] for o, *_ in mms)
                free[f"S{b}"] = add("dv", lambda e: e.tensor_reduce(mx[:, u, 4 * qt + h4, kb:kb + 1], Sb[b][:, 0:n], AX.X, ALU.max),
                               f"{tag}_mx", [p])
                last = i + 1 == len(stiles) or stiles[i + 1][0] != u
                if last:
                    nk = max(x[3] for x in stiles if x[0] == u) + 1
                    a = add("dv", lambda e: e.tensor_reduce(nm[:, u, :], mx[:, u, :, 0:nk], AX.X, ALU.max, negate=True),
                            f"{tag}_nm", [free[f"S{b}"]])
                    nv = nm[:, u, :]
                    rv = nr[:, u, :]
                    z = n3[:, u, :, :, :].rearrange("p q h s -> p (q h) s")
                    a = add("po", lambda e: e.tensor_copy(z[:, :, 0], nv), f"{tag}_n3", [a])
                    a = add("po", lambda e: e.tensor_tensor(rv, nv, z[:, :, 0], ALU.subtract), f"{tag}_n3", [a])
                    a = add("po", lambda e: e.tensor_copy(z[:, :, 1], rv), f"{tag}_n3", [a])
                    t_n3 = add("po", lambda e: e.tensor_tensor(z[:, :, 2], rv, z[:, :, 1], ALU.subtract), f"{tag}_n3", [a])

                    def turn():
                        Mh = Mb[:, :].bitcast(BF16)
                        for qt_ in range(4):
                            p = add("pe", lambda e, qt_=qt_: e.transpose(Mh[0:12, 128 * qt_:128 * qt_ + 128],
                                    n3[:, u, qt_, :, :].rearrange("p h s -> p (h s)"), idb[:, :]),
                                    f"{tag}_mT", [t_n3, free["M"], t_idb])
                        a = add("ac", lambda e: e.activation(nrow[:, u % 2, :], Mh[0:12, 0:CH], ACT.Copy), f"{tag}_nr",
                                [p, shift[u - 2] if u >= 2 else shift0[u % 2]])
                        free["M"] = a
                        for h4_ in range(4):
                            shift[u] = dma(shift_dst(u, h4_), nrow[3 * h4_:3 * h4_ + 3, u % 2, :], f"{tag}_sh{u}", [a])
                    at(J + 2, turn)

            shift0 = attention.shift_last
            pv_tok = {}
            ex_tok = {}

            def emit_st(j, pair):
                u, kt = steps[j]
                lo, mms = stmm(u, kt, pair)
                for m, (o, lt, rh, start, stop) in enumerate(mms):
                    p = add("pe", lambda e, o=o, lt=lt, rh=rh, start=start, stop=stop: e.matmul(
                        At[pair][:, o[0]:o[1]], lt, rh, start=start, stop=stop, skip_group_check=not start),
                        f"{tag}_T", [free[f"A{pair}"], shift[u]] + (st_ready(u) if m == 0 else []))
                slot = (2 * j + pair) % 4
                ai = At[pair][:, :].rearrange("p (i n) -> p i n", i=2)[:, :, lo:CH]
                ao = PT[slot][:, :].rearrange("p (i n) -> p i n", i=2)[:, :, lo:CH]
                t = add("ac", lambda e: e.activation(ao, ai, ACT.Exp), f"{tag}_ex", [p, pv_tok.get((j - 2, pair))])
                free[f"A{pair}"] = t
                ex_tok[(j, pair)] = t

            def emit_pv(j, pair):
                if j < 0:
                    return
                u, kt = steps[j]
                lo = width(u, kt)
                slot = (2 * j + pair) % 4
                for i in range(2):
                    g = 2 * pair + i
                    p = add("pe", lambda e, g=g, i=i: e.matmul(Ob[32 * g:32 * g + 32, lo:CH], vmm(u, kt, g),
                            PT[slot][:, CH * i + lo:CH * i + CH], start=(kt == 0), stop=True,
                            skip_group_check=(kt > 0), tile_position=(0, 32 * g)), f"{tag}_pv", [ex_tok[(j, pair)], free["O"], d_ready(u, kt)])
                pv_tok[(j, pair)] = p
                if kt == n_of[u] - 1 and pair == 1:
                    finish(u, j, p)

            def finish(u, j, p):
                c, quad = units[u]
                p_last = p
                prev = os_tok[u % 2]
                o = add("ac", lambda e: e.activation(Os[:, u % 2, :], Ob[:, :], ACT.Copy), f"{tag}_os", [p, prev])
                free["O"] = o

                def turn():
                    for qt in range(4):
                        p = add("pe", lambda e, qt=qt: e.transpose(Mb[:, 128 * qt:128 * qt + 128],
                                Os[:, u % 2, 128 * qt:128 * qt + 128], idf[:, :]), f"{tag}_oT", [o, free["M"]])
                    os_tok[u % 2] = p
                    Mq = Mb[:, :].rearrange("p (x w) -> p x w", w=32)
                    r = add("dv", lambda e: e.reciprocal(rl[:, u, :], Mq[:, :, dcols]), f"{tag}_rl", [p])
                    nq = 128 // (4 * dcols)
                    for qt in range(4):
                        w = add("dv", lambda e, qt=qt: e.tensor_tensor(
                            vw[:, c % 2, qt, 4 * dcols * quad:4 * dcols * quad + 4 * dcols].rearrange("p (g d) -> p g d", d=dcols),
                            Mq[:, 4 * qt:4 * qt + 4, 0:dcols],
                            rl[:, u, 4 * qt:4 * qt + 4].unsqueeze(2).to_broadcast([128, 4, dcols]), ALU.mult),
                            f"{tag}_vw", [r, vw_tok[c % 2]])
                    free["M"] = w
                    if quad == nq - 1:
                        def back():
                            for qt in range(4):
                                p = add("pe", lambda e, qt=qt: e.transpose(Mb[:, 128 * qt:128 * qt + 128],
                                        vw[:, c % 2, qt, :], idf[:, :]), f"{tag}_wT", [w, free["M"]])
                            vw_tok[c % 2] = p
                            a = add("ac", lambda e: e.activation(vwT[:, c % 2, :], Mb[:, :], ACT.Copy), f"{tag}_wc",
                                    [p, y_tok[c % 2]])
                            free["M"] = a
                            at(now[0] + 1, lambda: project(a))

                        def project(a):
                            for qt in range(4):
                                p = add("pe", lambda e, qt=qt: e.matmul(Mb[:, 128 * qt:128 * qt + 128],
                                        vwT[:, c % 2, 128 * qt:128 * qt + 128], wout[:, :], start=True, stop=True),
                                        f"{tag}_y", [a, t_wout])
                            y_tok[c % 2] = p
                            xv = xs[:, 4 * c:4 * c + 4, :]
                            x = add("dv", lambda e: e.tensor_tensor(xv, xv, Mb[:, :].rearrange("p (t n) -> p t n", t=4), ALU.add),
                                    f"{tag}_x", [p, ("po_xb", counts["po_xb"])])
                            free["M"] = x
                            x_done[c] = x
                            if on_chunk:
                                on_chunk(c, x, p_last, at, now[0])
                        at(now[0] + 1, back)
                at(now[0] + 2, turn)

            os_tok, vw_tok, y_tok = attention.os_tok, attention.vw_tok, attention.y_tok
            now = [-2]
            for J0, fn in hooks:
                at(J0, fn)

            def do_later():
                while True:
                    ks = [k for k in later if k <= now[0]]
                    if not ks:
                        break
                    for k in sorted(ks):
                        for fn in later.pop(k):
                            fn()

            cum = 0
            for J in range(len(steps) + 1):
                now[0] = J
                if J < len(steps):
                    u = steps[J][0]
                    nxt = n_of[u + 1] if u + 1 < nU else 0
                    target = min(4 * (J + nxt + 5), len(stiles))
                else:
                    target = len(stiles)
                k = max(0, target - state["si"])
                if J == 0:
                    first = len([1 for x in stiles if x[0] == 0])
                    for fn in before:
                        if callable(fn):
                            fn()
                        else:
                            for _ in range(fn):
                                emit_s(-2)
                    while state["si"] < first:
                        emit_s(-2)
                    for _ in range(max(0, target - state["si"] - 4)):
                        emit_s(-2)
                    k = max(0, target - state["si"])
                do_later()
                parts = [k // 4 + (1 if i < k % 4 else 0) for i in range(4)]
                for i in range(4):
                    for _ in range(parts[i]):
                        emit_s(J)
                    if i % 2 == 0:
                        if J < len(steps):
                            emit_st(J, i // 2)
                    else:
                        emit_pv(J - 1, i // 2)
            while later:
                now[0] += 1
                do_later()
            attention.shift_last = [shift[nU - 2], shift[nU - 1]] if nU % 2 == 0 else [shift[nU - 1], shift[nU - 2]]
            attention.last_pv = pv_tok[(len(steps) - 1, 1)]
            attention.last_ex = [free["A0"], free["A1"]]
            return x_done

        attention.shift_last = [None, None]
        attention.os_tok, attention.vw_tok, attention.y_tok = [None, None], [None, None], [None, None]

        units0 = [(c, q) for c in range(4) for q in range(4)]

        def s0(u, _):
            c, quad = units0[u]
            r = []
            order = [(qt, kb) for kb in range(4) for qt in range(4)] if u == 0 else [(qt, kb) for qt in range(4) for kb in range(4)]
            for qt, kb in order:
                for h4 in range(4):
                    hd = 4 * quad + h4
                    q0 = CH * (c % 2) + 128 * qt
                    r.append((qt, h4, kb, [((0, CH), Qs[0:96, hd, q0:q0 + 128], Ks[0:96, hd // 2, CH * kb:CH * kb + CH], True, True)]))
            return r

        def st0(u, kt, pair):
            c, quad = units0[u]
            q0 = CH * (c % 2)
            return 0, [((CH * i, CH * i + CH), Ks[0:99, (4 * quad + 2 * pair + i) // 2, 128 * kt:128 * kt + 128],
                        Qs[0:99, 4 * quad + 2 * pair + i, q0:q0 + CH], True, True) for i in range(2)]

        def sh0(u, h4):
            c, quad = units0[u]
            return Qs[96:99, 4 * quad + h4, CH * (c % 2):CH * (c % 2) + CH]

        def next_q(c, x, p, at, now):
            if c + 2 < 4:
                q_free[c + 2] = [p]
                at(now + 1, lambda: project_q(c + 2))

        setup0(0)
        t_k1 = add("dv", lambda e: e.memset(Ks[96:128, :, :].bitcast(mybir.dt.uint32), 0x3F803F80), "c2")
        setup0(1)
        before0 = [16, lambda: setup0(2), 16, lambda: setup0(3), 16, lambda: [output_bias0(c) for c in range(4)]]
        xd0 = attention(0, units0, s0, st0, lambda u, kt, g: Va[:, kt, 4 * units0[u][1] + g, :],
                        lambda u, kt: 16 if kt is None else 0, 8, lambda u, kt: t_v[kt // 4], sh0, woT, t_wo, None,
                        lambda u, kb: [t_k[kb], t_q[units0[u][0]]],
                        lambda u: [t_k1, t_q[units0[u][0]]],
                        before=before0, hooks=[(3, lambda: project_q(1))], on_chunk=next_q)
        pv0 = attention.last_pv

        mkd = [PT[0][:, 0:CH], PT[0][:, CH:], PT[1][:, 0:CH], PT[1][:, CH:]]
        ams = [PT[2][:, 0:CH], PT[2][:, CH:], PT[3][:, 0:CH], PT[3][:, CH:]]
        Gp, Up, Gs_, Us_ = A0, A1, A2, A3
        Vf = Va[:, :, :, :].rearrange("p k h w -> p (k h w)")
        bt = Vf[:, 0:1024].rearrange("p (a n) -> p a n", a=2)
        bsg = Vf[:, 1024:2048].rearrange("p (a n) -> p a n", a=2)
        hs = Vf[:, 2048:2560]
        F = {"mk": [pv0] * 4, "am": [pv0] * 4, "mask": [None] * 16, "bt": [None, None], "bsg": [None, None], "hs": None}
        gfree = {"G": [free["A0"]], "H": [free["A1"]]}
        xd1 = {}

        def mbs(n):
            return Ks[:, n // 4, CH * (n % 4):CH * (n % 4) + CH]

        def silu_mul(G, U, key, p, dst, dst_free, k):
            a = add("ac", lambda e: e.activation(bsg[:, k, :], G, ACT.Sigmoid), "ff_sg", [p, F["bsg"][k]])
            b = add("dv", lambda e: e.tensor_tensor(bt[:, k, :], G, bsg[:, k, :], ALU.mult), "ff_d", [a, F["bt"][k]])
            F["bsg"][k] = b
            d = add("dv", lambda e: e.tensor_tensor(dst, U, bt[:, k, :], ALU.mult), "ff_d", [b, dst_free])
            F["bt"][k] = d
            gfree[key] = [d]
            return d

        t_E = add("dv", lambda e: e.tensor_copy(E, idf[0:16, 0:16].unsqueeze(2).to_broadcast([16, 16, 128])), "ff_E", [t_id])
        t_q1, t_kk, t_v1s, h1 = [], [], [], []

        def setup1a(c, bank, key):
            h1.append(ln(c, 1, False, bank, key, xd1[c], F["down"][c]))
            add("po", lambda e: e.tensor_tensor(xs[:, 4 * c:4 * c + 4, :], xs[:, 4 * c:4 * c + 4, :],
                bpB[:, :].unsqueeze(1).to_broadcast([128, 4, 128]), ALU.add), "po_xb", [h1[c][1]])

        def setup1b(c, bank, key):
            h = h1[c][0]
            cols = slice(CH * c, CH * c + CH)

            def place_k(parts, g):
                scr = scratch["k1"][:, :, cols]
                tw = store_rows("k", scr, parts, f"k1w{c}", g)
                return [tw, dma(Ks[0:96, 7, cols], scr.rearrange("j d n -> (j d) n"), f"k1{c}", [tw, pv0])]

            def place_q(parts, g):
                scr = scratch["q1"][:, :, cols]
                tw = store_rows("q", scr, parts, f"q1w{c}", g)
                return [tw, dma(Q1[0:96, :, cols], scr.rearrange("j (d h) n -> (j d) h n", h=8), f"q1{c}", [tw, pv0])]

            p = add("pe", lambda e: e.matmul(bank[0:16, :], wk1[:, :], hc(c), start=True, stop=True), "pe_p1", [h, free[key]])
            t_kk.append(split(bank, key, p, 16, None, 1.0, place_k)[1])
            p = add("pe", lambda e: e.matmul(bank[:, :], wq1[:, :], hc(c), start=True, stop=True), "pe_p1", [free[key]])
            t_q1.append(split(bank, key, p, 128, None, 128.0 ** -0.5, place_q)[1])
            for j in range(4):
                p = add("pe", lambda e, j=j: e.matmul(bank[:, 128 * j:128 * j + 16], hc(c, 128 * j, 128 * j + 128), wv1[:, :],
                                                      start=True, stop=True), "pe_p1", [free[key]])
            t = add("dv", lambda e: e.tensor_copy(V1[:, 4 * c:4 * c + 4, 0:16], bank[:, :].rearrange("p (t n) -> p t n", t=4)[:, :, 0:16]),
                    "dv_v", [p, t_v1])
            free[key] = t
            t_v1s.append(t)

        F["down"] = {}
        hx = {}
        hx[0] = ln(0, 0, True, Sb[0][:, :], "S0", xd0[0], hts[0][0])
        def experts(c):
            h = hx[c][0]
            for j in range(4):
                p = add("pe", lambda e, c=c, j=j: e.matmul(Mb[:, 16 * j:16 * j + 16], hc(c, 128 * j, 128 * j + 128), rwT[:, :],
                                                           start=True, stop=True), "ff_lg", [h, free["M"], l1])
            a = add("dv", lambda e: e.tensor_copy(lg, Mb[:, 0:64].rearrange("p (t n) -> p t n", t=4)), "ff_r", [p])
            free["M"] = a
            a = add("dv", lambda e: e.tensor_reduce(lm[:, :], lg, AX.X, ALU.max), "ff_r", [a])
            sg = add("ac", lambda e: e.activation(sgm[:, :], lm[:, :], ACT.Sigmoid), "ff_sm", [a])
            a = add("dv", lambda e: e.tensor_tensor(eq, lg, lm[:, :].unsqueeze(2).to_broadcast([128, 4, 16]), ALU.is_equal), "ff_r", [a])
            a = add("dv", lambda e: e.tensor_tensor(wv_, eq, desc[:, :].unsqueeze(1).to_broadcast([128, 4, 16]), ALU.mult), "ff_r", [a])
            a = add("dv", lambda e: e.tensor_reduce(wm[:, :], wv_, AX.X, ALU.max), "ff_r", [a])
            a = add("dv", lambda e: e.tensor_tensor(oh, wv_, wm[:, :].unsqueeze(2).to_broadcast([128, 4, 16]), ALU.is_equal), "ff_r", [a])
            b = add("dv", lambda e: e.tensor_copy(ohb[:, :, :], oh), "ff_r", [a])
            b = add("dv", lambda e: e.tensor_tensor(soh, oh, sgm[:, :].unsqueeze(2).to_broadcast([128, 4, 16]), ALU.mult), "ff_r", [a, sg])

            sh_toks = []
            shb = []

            def shared_block(bl):
                key = "GH"[bl % 2]
                G, U = ((Gp, Up), (Gs_, Us_))[bl % 2]
                for W, O_ in ((sgT, G), (suT, U)):
                    p = add("pe", lambda e, W=W, O_=O_: e.matmul(O_, W[:, 128 * bl:128 * bl + 128], hc(c), start=True, stop=True),
                            "ff_sh", [h] + gfree[key])
                sh_toks.append((bl, silu_mul(G, U, key, p, ams[bl], F["am"][bl], bl % 2)))

            for bl in range(4):
                shared_block(bl)
                if bl == 1:
                    Mh = Mb[:, :].bitcast(BF16)
                    for j in range(4):
                        p = add("pe", lambda e, j=j: e.transpose(Mh[0:16, 128 * j:128 * j + 128], ohb[:, j, :], idb[:, :]), "ff_tr", [b, free["M"]])
                    a = add("dv", lambda e: e.tensor_copy(ohT, Mh[0:16, 0:CH]), "ff_o", [p])
                    for j in range(4):
                        p = add("pe", lambda e, j=j: e.transpose(Sb[1][0:16, 128 * j:128 * j + 128], soh[:, j, :], idf[:, :]), "ff_tr", [b, free["S1"]])
                    a2 = add("dv", lambda e: e.tensor_copy(sT, Sb[1][0:16, :]), "ff_o", [p])
                    p = add("pe", lambda e: e.matmul(Mb[:, :], onesf[0:16, :], sT, start=True, stop=True), "ff_sb", [a, a2, t_one])
                    t_hs = add("dv", lambda e, c=c: e.tensor_tensor(hs, hc(c), Mb[:, :], ALU.mult), "ff_o", [p, h])
                    free["M"] = t_hs
                    free["S1"] = a2
            if c > 0:
                setup1a(c - 1, Sb[0][:, :], "S0")
            first_y = [True]

            def down(am, w, tok, sig="ff_y"):
                for j in range(4):
                    p = add("pe", lambda e, j=j, s=first_y[0] and j == 0: e.matmul(Ob[:, 128 * j:128 * j + 128], am[:, 128 * j:128 * j + 128], w,
                                                     start=s, stop=True, skip_group_check=True), sig, [tok, free["O"], t_dn])
                first_y[0] = False
                return p
            exp_banks = [("S1", Sb[1]), ("M", Mb)]
            mtoks = {}

            def mask(n):
                key, bank = exp_banks[n % 2]
                p = add("pe", lambda e: e.matmul(bank[:, :], E[:, n, :], ohT, start=True, stop=True), "ff_mb", [free[key], a, t_E])
                cpy = add("ac", lambda e: e.activation(mbs(n), bank[:, :], ACT.Copy), "ff_mc", [p, F["mask"][n], pv0])
                k = n % 4
                m_ = add("dv", lambda e: e.tensor_tensor(mkd[k], hs, bank[:, :], ALU.mult), "ff_mk", [cpy, t_hs, F["mk"][k]])
                free[key] = m_
                mtoks[n] = (m_, cpy)

            mask(0)
            mask(1)
            for bl, tok in sh_toks:
                F["am"][bl] = down(ams[bl], sdT[:, bl, :], tok)
                if bl < 2:
                    mask(2 + bl)
            for n in range(16):
                for W, O_ in ((0, Gp), (128, Up)):
                    p = add("pe", lambda e, W=W, O_=O_, n=n: e.matmul(O_, gu[:, n, W:W + 128], mkd[n % 4], start=(n == 0), stop=(n == 15)),
                            "ff_e", [mtoks[n][0]] + gfree["G"] + gfree["H"])
                F["mk"][n % 4] = p
                if n + 4 < 16:
                    mask(n + 4)
            d = silu_mul(Gp, Up, "G", p, hs, None, 0)
            if c > 0:
                setup1b(c - 1, Sb[0], "S0")
            if c < 3:
                hx[c + 1] = ln(c + 1, 0, True, Sb[0][:, :], "S0", xd0[c + 1], hts[c + 1][0])
            for n in range(16):
                k = n % 4
                eng = "po" if n % 3 == 1 else "dv"
                m_ = add(eng, lambda e, n=n, k=k: e.tensor_tensor(ams[k], hs, mbs(n), ALU.mult), "ff_am_" + eng, [d, mtoks[n][1], F["am"][k]])
                F["mask"][n] = m_
                F["am"][k] = down(ams[k], dn[:, n, :], m_)
            xv = xs[:, 4 * c:4 * c + 4, :]
            x = add("dv", lambda e, xv=xv: e.tensor_tensor(xv, xv, Ob[:, :].rearrange("p (t n) -> p t n", t=4), ALU.add),
                    "ff_x", [F["am"][3]])
            free["O"] = x
            xd1[c] = x
            F["down"][c] = F["am"][3]

        for c in range(4):
            experts(c)
        free["A0"] = free["A1"] = gfree["G"][0]

        units1 = [(c, q) for c in range(4) for q in range(2)]

        def s1(u, _):
            c, quad = units1[u]
            r = []
            for qt in range(4):
                for kb in range(c + 1):
                    for h4 in range(4):
                        qap = Q1[0:96, 4 * quad + h4, CH * c + 128 * qt:CH * c + 128 * qt + 128]
                        n = CH if kb < c else 128 * (qt + 1)
                        m = [((0, n), qap, Ks[0:96, 7, CH * kb:CH * kb + n], True, True)]
                        if kb == c:
                            m.append(((n - 128, n), idb[:, :], mq[:, :], False, True))
                        r.append((qt, h4, kb, m))
            return r

        def st1(u, kt, pair):
            c, quad = units1[u]
            lo = width1(u, kt)
            diag = kt >= 4 * c
            r = []
            for i in range(2):
                hd = 4 * quad + 2 * pair + i
                r.append(((CH * i + lo, CH * i + CH), Ks[0:99, 7, 128 * kt:128 * kt + 128],
                          Q1[0:99, hd, CH * c + lo:CH * c + CH], True, True))
                if diag:
                    r.append(((CH * i + lo, CH * i + lo + 128), idb[:, :], mk[:, :], False, True))
            return lo, r

        def width1(u, kt):
            c = units1[u][0]
            if kt is None:
                return 4 * (c + 1)
            return max(0, 128 * (kt - 4 * c))

        mixed = {}
        mt = Vf[:, 3072:3072 + 10 * CH].rearrange("p (a n) -> p a n", n=CH)

        def mix_start(c, x, p, at, now):
            s = 5 * (c % 2)
            xr, xk, kr, sr, vv = (mt[:, s + i, :] for i in range(5))
            hp = hT[:, CH * c:CH * c + CH]
            old = mixed.get(c - 2)

            def a0():
                mixed[c, "h"] = ln(c, 1, True, Mb[:, :], "M", x, h1[c][0])

            def a1():
                h = mixed[c, "h"][0]
                hb = mixed[max(c - 1, 0), "h"][0]
                add("dv", lambda e: e.tensor_scalar(xr, hc(c), mur[:, 0:1], None, ALU.mult), "cm_d", [h, hb, old, t_om])
                d = add("dv", lambda e: e.tensor_scalar(xk, hc(c), muk[:, 0:1], None, ALU.mult), "cm_d")
                d = add("dv", lambda e: e.scalar_tensor_tensor(xk, hp, omk[:, 0:1], xk, ALU.mult, ALU.add), "cm_d", [d])
                d2 = add("dv", lambda e: e.scalar_tensor_tensor(xr, hp, omr[:, 0:1], xr, ALU.mult, ALU.add), "cm_d")
                p = add("pe", lambda e: e.matmul(Mb[:, :], wkk[:, :], xk, start=True, stop=True), "cm_p", [d, free["M"]])
                a = add("dv", lambda e: e.tensor_scalar(kr, Mb[:, :], 0.0, None, ALU.max), "cm_d", [p])
                free["M"] = a
                mixed[c, "d"] = d2
                mixed[c, "k"] = add("dv", lambda e: e.tensor_tensor(kr, kr, kr, ALU.mult), "cm_d", [a])

            def a2():
                for j in range(4):
                    p = add("pe", lambda e, j=j: e.matmul(Mb[:, 128 * j:128 * j + 128], xr[:, 128 * j:128 * j + 128], wr[:, :],
                                                          start=True, stop=True), "cm_p", [mixed[c, "d"], free["M"]])
                free["M"] = mixed[c, "s"] = add("ac", lambda e: e.activation(sr, Mb[:, :], ACT.Sigmoid), "cm_a", [p])

            def a3():
                for j in range(4):
                    p = add("pe", lambda e, j=j: e.matmul(Mb[:, 128 * j:128 * j + 128], kr[:, 128 * j:128 * j + 128], wvv[:, :],
                                                          start=True, stop=True), "cm_p", [mixed[c, "k"], free["M"], t_wvv])
                a = add("dv", lambda e: e.tensor_tensor(vv, sr, Mb[:, :], ALU.mult), "cm_d", [p, mixed[c, "s"]])
                free["M"] = a
                mixed[c] = a
                xv = xs[:, 4 * c:4 * c + 4, :]
                a = add("dv", lambda e: e.tensor_tensor(xv, xv, vv.rearrange("p (t n) -> p t n", t=4), ALU.add), "cm_d",
                        [a, mixed[c, "h"][1]])
                mixed["out"] = dma(out.rearrange("a (t p) n -> p (a t) n", p=128)[:, 4 * c:4 * c + 4, :], xv, "st_out", [a])

            for k, fn in enumerate((a0, a1, a2, a3)):
                at(now + 1 + k, fn)

        attention(1, units1, s1, st1, lambda u, kt, g: V1[:, kt, :], width1, 16, lambda u, kt: t_v1s[kt // 4],
                  lambda u, h4: Q1[96:99, 4 * units1[u][1] + h4, CH * units1[u][0]:CH * units1[u][0] + CH],
                  wp1, t_wp, None,
                  lambda u, kb: [t_kk[kb], t_q1[units1[u][0]]],
                  lambda u: [t_k1, t_q1[units1[u][0]]] + t_kk[0:units1[u][0] + 1],
                  hooks=[(1, lambda: setup1a(3, Mb[:, :], "M")), (3, lambda: setup1b(3, Mb, "M"))], on_chunk=mix_start)
        t_out = mixed["out"]
        queues["sp"].append((None, None, 0, [t_out]))

        block = ctx.enter_context(nc.Block())

        @block.sync
        def _(e):
            tail = queues["sp"].pop()
            run("sp", e)
            for s, v in tail[3]:
                e.wait_ge(sems[s], v)

        @block.tensor
        def _(e):
            run("pe", e)

        @block.vector
        def _(e):
            run("dv", e)

        @block.scalar
        def _(e):
            run("ac", e)

        @block.gpsimd
        def _(e):
            run("po", e)


_TURNED = ('L0_attn_Wq', 'L0_attn_Wk', 'L0_attn_Wv', 'L0_attn_Wo', 'L0_ffn_router_w', 'L0_ffn_shared_gate_w',
           'L0_ffn_shared_up_w', 'L0_ffn_shared_down_w', 'L1_ffn_W_r', 'L1_ffn_W_k', 'L1_ffn_W_v')


def kernel(**inputs):
    import numpy as _np
    import concourse.bacc as _bacc
    from concourse import mybir as _mybir
    from concourse.bass_utils import run_bass_kernel_spmd as _run

    nc = _bacc.Bacc("TRN2", target_bir_lowering=False, num_devices=1)
    arrays, args = {}, {}
    for name in inputs:
        a = _np.asarray(inputs[name])
        if name in ('L0_attn_Wq', 'L0_attn_Wk', 'L0_attn_bq', 'L0_attn_bk'):
            a = a.reshape(8, 2, 8, -1).transpose(2, 1, 0, 3).reshape(a.shape)
        if name == 'L1_attn_Wq':
            a = a.transpose(1, 2, 0)
        a = _np.ascontiguousarray(a.T if name in _TURNED else a)
        arrays[f"in_{name}"] = a
        args[name] = nc.dram_tensor(f"in_{name}", a.shape, _mybir.dt.from_np(a.dtype), kind="ExternalInput").ap()
    o = nc.dram_tensor("out_0", (1, 2048, 128), _mybir.dt.float32, kind="ExternalOutput").ap()
    adaln_two_layers(nc, args, o)
    r = _run(nc, [arrays], core_ids=[0])
    return r.results[0]["out_0"]
```

```python
import concourse.bass as bass
from concourse import mybir
from contextlib import ExitStack

F32 = mybir.dt.float32
BF16 = mybir.dt.bfloat16
ALU = mybir.AluOpType
ACT = mybir.ActivationFunctionType
AX = mybir.AxisListType

S = 2048
NC_ = 4
CH = 512
EPS = 1e-5
NEG = -1e30
LEAD = 4
NT = 31
PW = 129
U32 = mybir.dt.uint32
I32 = mybir.dt.int32


def adaln_two_layers(nc, A, out):
    ctx = ExitStack()
    with ctx:
        def sb(name, shape, dt=F32):
            return ctx.enter_context(nc.sbuf_tensor(name, shape, dt))

        def pb(name, shape):
            return ctx.enter_context(nc.psum_tensor(name, shape, F32))

        queues = {"pe": [], "dv": [], "ac": [], "po": [], "sp": []}
        sems, counts = {}, {}

        def sem(name):
            if name not in sems:
                sems[name] = ctx.enter_context(nc.semaphore(name))
                counts[name] = 0
            return sems[name]

        def add(eng, fn, sig=None, after=(), by=1):
            tok = None
            if sig is not None:
                sem(sig)
                counts[sig] += by
                tok = (sig, counts[sig])
            queues[eng].append((fn, sig, by, [t for t in after if t is not None]))
            return tok

        def dma(dst, src, sig, after=(), eng="sp"):
            return add(eng, lambda e: e.dma_start(dst, src), sig, after, by=16)

        def run(name, e):
            seen = {}
            for fn, sig, by, after in queues[name]:
                for s, v in after:
                    if seen.get(s, 0) < v:
                        e.wait_ge(sems[s], v)
                        seen[s] = v
                ins = fn(e)
                if sig is not None:
                    ins.then_inc(sems[sig], by)

        Qs = sb("Qs", [128, 16, 2 * CH], BF16)
        Q1 = Qs[:, :, :].rearrange("p h n -> p (h n)").rearrange("p (h n) -> p h n", h=8)
        Ks = sb("Ks", [128, 8, S], BF16)
        Va = sb("Va", [128, 16, 16, 32])
        V1 = sb("V1", [128, 16, 32])
        xs = sb("xs", [128, 16, 128])
        hT = sb("hT", [128, 1 + S])
        xh = sb("xh", [128, 8, 128])
        PT = [sb(f"PT{i}", [128, 1024]) for i in range(4)]
        qf = sb("qf", [128, 2, CH])
        q3 = sb("q3", [128, 2, 3, CH], BF16)
        st = sb("st", [128, 16, 6])
        mv = sb("mv", [128, 16, 2])
        ve = sb("ve", [128, 16])
        rs = sb("rs", [128, 16])
        mh = sb("mh", [128, 4])
        Os = sb("Os", [128, 2, CH])
        rl = sb("rl", [128, 16, 16])
        vw = sb("vw", [128, 2, 4, 128])
        vwT = sb("vwT", [128, 2, CH])
        mxr = sb("mx", [128, 1024])
        mx = mxr[:, :].rearrange("p (u q k) -> p u q k", u=16, k=4)
        nm = sb("nm", [128, 16, 16])
        nr = sb("nr", [128, 16, 16])
        n3 = sb("n3", [128, 16, 4, 4, 3], BF16)
        nrow = sb("nrow", [12, 2, CH], BF16)
        idf = sb("idf", [128, 128])
        idb = sb("idb", [128, 128], BF16)
        mq = sb("mq", [128, 128], BF16)
        mk = sb("mk", [128, 128], BF16)
        onesf = sb("onesf", [128, 128])
        wqT, wkT, wvT, woT = (sb(n, [128, 128]) for n in ("wqT", "wkT", "wvT", "woT"))
        bq, bk, bqs = (sb(n, [128, 1]) for n in ("bq", "bk", "bqs"))
        bvB, boB, bpB = (sb(n, [128, 128]) for n in ("bvB", "boB", "bpB"))
        rwT = sb("rwT", [128, 16])
        XP = sb("XP", [128, 16, PW])
        OH = sb("OH", [128, 16, 16])
        OHb = sb("OHb", [128, 16, 16], BF16)
        Ub = sb("Ub", [128, 128], BF16)
        onesb = sb("onesb", [128, 128], BF16)
        LT = sb("LT", [128, 16, 16])
        iti = sb("iti", [128, 33], I32)
        itf = sb("itf", [128, 33])
        k128 = sb("k128", [128, 16])
        posu = sb("posu", [128, 16], U32)
        idxu = sb("idxu", [128, NT], U32)
        sgT, suT = sb("sgT", [128, CH]), sb("suT", [128, CH])
        sdT = sb("sdT", [128, 4, 128])
        wk1, wv1 = sb("wk1", [128, 16]), sb("wv1", [128, 16])
        wq1 = sb("wq1", [128, 128])
        wp1 = sb("wp1", [128, 128])
        wr, wkk, wvv = (sb(n, [128, 128]) for n in ("wr", "wkk", "wvv"))
        mur, muk, omr, omk = (sb(n, [128, 1]) for n in ("mur", "muk", "omr", "omk"))
        desc = sb("desc", [128, 16])
        mods = []
        cc = sb("cc", [128, 2])
        csg = sb("csg", [128, 2])
        cs = sb("cs", [128, 2])
        mc = sb("mc", [128, 2, 4])
        gB = sb("gB", [128, 4, 128])
        rt = sb("rt", [128, 12, 16])
        lg, eq, wv_ = (rt[:, 4 * i:4 * i + 4, :] for i in range(3))
        lm = sb("lm", [128, 16])
        wm = sb("wm", [128, 4])

        At = [pb("At0", [128, 1024]), pb("At1", [128, 1024])]
        Sb = [pb("Sb0", [128, CH]), pb("Sb1", [128, CH])]
        Ob = pb("Ob", [128, CH])
        Mb = pb("Mb", [128, CH])
        A0, A1, A2, A3 = (At[i // 2][:, CH * (i % 2):CH * (i % 2) + CH] for i in range(4))


        sorted_x = nc.dram_tensor("sorted_x", [NT * 128, PW], F32).ap()
        sorted_y = nc.dram_tensor("sorted_y", [NT * 128, 128], F32).ap()
        scratch = {n: nc.dram_tensor(f"rows_{n}", [6, 16 if n == "k1" else 128, S], BF16).ap() for n in ("q", "k", "q1", "k1")}

        xd = A["L0_attn_x"].rearrange("a (t p) n -> p (a t) n", p=128)

        def col(v):
            return v.rearrange("(n a) -> n a", a=1)

        XPf = XP[:, :, :].rearrange("p t n -> p (t n)")
        wm_sb = [XPf[:, 129:897], XPf[:, 897:1665]]
        cb = XPf[:, 1665:1921].rearrange("p (i n) -> p i n", i=2)
        gt = vw[:, :, :, :].rearrange("p a g n -> p (a g n)")
        lx = [dma(xs[:, 0:4, :], xd[:, 0:4, :], "ld_x0")]
        dma(cc[:, 0:1], A["L0_c"].rearrange("a n -> n a"), "ld_c", eng="ac")
        lc = dma(cc[:, 1:2], A["L1_c"].rearrange("a n -> n a"), "ld_c", eng="ac")
        lwa = dma(wm_sb[0][:, 0:256], A["L0_wmod"][:, 0:256], "ld_wa", eng="ac")
        lx.append(dma(xs[:, 4:8, :], xd[:, 4:8, :], "ld_x1"))
        for dst, src in ((wkT, A["L0_attn_Wk"]), (wqT, A["L0_attn_Wq"])):
            l0 = dma(dst[:, :], src, "ld_w0")
        for dst, src in ((bk, "L0_attn_bk"), (bq, "L0_attn_bq")):
            l0 = dma(dst[:, :], col(A[src]), "ld_w0")
        lx += [dma(xs[:, 4 * c:4 * c + 4, :], xd[:, 4 * c:4 * c + 4, :], f"ld_x{c}") for c in (2, 3)]
        dma(wvT[:, :], A["L0_attn_Wv"], "ld_wv")
        lv = dma(bvB[:, :], A["L0_attn_bv"].partition_broadcast(128), "ld_wv")
        dma(wm_sb[0][:, 256:768], A["L0_wmod"][:, 256:768], "ld_wm")
        lw = dma(wm_sb[1][:, 0:768], A["L1_wmod"], "ld_wm")

        def load_rest():
            for dst, src in ((woT[:, :], A["L0_attn_Wo"]),
                             (boB[:, :], A["L0_attn_bo"].partition_broadcast(128)),
                             (bpB[:, :], A["L1_attn_bp"].partition_broadcast(128)),
                             (rwT[:, :], A["L0_ffn_router_w"]),
                             (sgT[:, :], A["L0_ffn_shared_gate_w"]), (suT[:, :], A["L0_ffn_shared_up_w"]),
                             (sdT[:, :, :], A["L0_ffn_shared_down_w"].rearrange("(b f) h -> f b h", f=128)),
                             (wk1[:, :], A["L1_attn_Wk"]), (wv1[:, :], A["L1_attn_Wv"]),
                             (wq1[:, :], A["L1_attn_Wq"].rearrange("c d q -> c (d q)")),
                             (wp1[:, :], A["L1_attn_Wp"]),
                             (wr[:, :], A["L1_ffn_W_r"]), (wkk[:, :], A["L1_ffn_W_k"]), (wvv[:, :], A["L1_ffn_W_v"]),
                             (mur[:, :], col(A["L1_ffn_mu_r"])), (muk[:, :], col(A["L1_ffn_mu_k"]))):
                t = dma(dst, src, "ld_w1")
            return t

        free = {k: None for k in ("M", "O", "S0", "S1", "A0", "A1")}
        t_mh = add("po", lambda e: e.memset(mh[:, :], -0.5), "c1")
        c0 = add("po", lambda e: e.memset(idf[:, :], 0.0), "c0")
        t_id = add("po", lambda e: e.affine_select(out=idf[:, :], in_=idf[:, :], compare_op=ALU.not_equal, fill=1.0,
                                                   base=0, pattern=[[-1, 128]], channel_multiplier=1), "c1", [c0])
        t_one = add("po", lambda e: e.memset(hT[:, 0:1], 0.0), "c1")
        c2 = add("dv", lambda e: e.memset(onesf[:, :], 1.0), "c2")
        t_qz = [add("dv", lambda e: e.memset(Qs[:, :, 0:CH].bitcast(F32), 0.0), "c2")]
        t_va = [add("po", lambda e: e.memset(Va[:, 0:4, :, :], 1.0), "c4")]

        def more_constants():
            add("po", lambda e: e.memset(mq[:, :], 0.0), "c0")
            c0 = add("po", lambda e: e.memset(mk[:, :], 0.0), "c0")
            add("po", lambda e: e.affine_select(out=mq[:, :], in_=mq[:, :], compare_op=ALU.is_ge, fill=NEG,
                                                base=0, pattern=[[-1, 128]], channel_multiplier=1), "c1", [c0])
            add("po", lambda e: e.affine_select(out=mk[:, :], in_=mk[:, :], compare_op=ALU.is_ge, fill=NEG,
                                                base=0, pattern=[[1, 128]], channel_multiplier=-1), "c1")
            add("po", lambda e: e.iota(iti[:, 0:32], [[1, 32]], base=0, channel_multiplier=0), "c5")
            add("po", lambda e: e.iota(iti[:, 32:33], [[1, 1]], base=0, channel_multiplier=1), "c5")
            add("po", lambda e: e.memset(Ub[:, :], 1.0), "c5")
            add("po", lambda e: e.memset(onesb[:, :], 1.0), "c5")
            c5 = add("po", lambda e: e.memset(XP[:, 0, :], 0.0), "c5")
            t_ub = add("po", lambda e: e.affine_select(out=Ub[:, :], in_=Ub[:, :], compare_op=ALU.is_gt, fill=0.0,
                                                       base=0, pattern=[[1, 128]], channel_multiplier=-1), "c5", [c5])
            t_zx = dma(sorted_x.rearrange("(i p) n -> p i n", p=128), XP[:, 0:1, :].to_broadcast([128, NT, PW]), "zx", [c5], eng="po")
            return t_ub, t_zx

        def late_constants():
            t_v1 = add("dv", lambda e: e.memset(V1[:, :, :], 1.0), "c2")
            for n in range(16):
                t_de = add("dv", lambda e, n=n: e.memset(desc[:, n:n + 1], float(16 - n)), "c2")
            t_it = add("dv", lambda e: e.tensor_copy(itf[:, :], iti[:, :]), "dv_it", [t_ub])
            add("dv", lambda e: e.tensor_scalar(k128[:, :], itf[:, 0:16], 128.0, None, ALU.mult), "dv_it", [t_it])
            t_it = add("dv", lambda e: e.tensor_tensor(LT[:, :, :], itf[:, 0:16].unsqueeze(2).to_broadcast([128, 16, 16]),
                                                       itf[:, 0:16].unsqueeze(1).to_broadcast([128, 16, 16]), ALU.is_gt), "dv_it", [t_it])
            add("dv", lambda e: e.tensor_scalar(omr[:, :], mur[:, :], -1.0, 1.0, ALU.mult, ALU.add), "dv_om", [l1])
            t_om = add("dv", lambda e: e.tensor_scalar(omk[:, :], muk[:, :], -1.0, 1.0, ALU.mult, ALU.add), "dv_om")
            R.update(v1=t_v1, desc=t_de, it=t_it, om=t_om)

        tmc = {}

        def mod_silu():
            t = add("ac", lambda e: e.activation(csg[:, :], cc[:, :], ACT.Sigmoid), "ac_set", [lc])
            return add("dv", lambda e: e.tensor_tensor(cs[:, :], cc[:, :], csg[:, :], ALU.mult), "dv_set", [t, lc])

        def mod_columns(items, ready):
            for i, k in items:
                j = (0, 1, 3, 4)[k]
                tm = add("pe", lambda e, i=i, j=j, k=k: e.matmul(Mb[:, 4 * i + k:4 * i + k + 1],
                         wm_sb[i][:, 128 * j:128 * j + 128], cs[:, i:i + 1], start=True, stop=True),
                         "pe_set", [ready, tcs, free["M"]])
            for i in range(2):
                ks = [k for i_, k in items if i_ == i]
                if not ks:
                    continue
                o = 4 * i + ks[0]
                t = add("dv", lambda e, i=i, o=o, ks=ks: e.tensor_copy(mc[:, i, ks[0]:ks[-1] + 1], Mb[:, o:o + len(ks)]), "dv_set", [tm])
                t = add("dv", lambda e, i=i, ks=ks: e.tensor_scalar(mc[:, i, ks[0] + 1:ks[-1] + 1:2], mc[:, i, ks[0] + 1:ks[-1] + 1:2],
                                                                    1.0, None, ALU.add), "dv_set", [t])
                free["M"] = t
                for k in ks:
                    tmc[i, k] = t

        def gates():
            for i in range(2):
                t = add("dv", lambda e, i=i: e.tensor_scalar(cb[:, i, :], onesf[:, :], cs[:, i:i + 1], None, ALU.mult),
                        "dv_set", [tcs, c2])
            for i in range(2):
                for k, j in enumerate((2, 5)):
                    g = 2 * i + k
                    tm = add("pe", lambda e, i=i, j=j, g=g: e.matmul(Mb[:, 128 * g:128 * g + 128],
                             cb[:, i, :], wm_sb[i][:, 128 * j:128 * j + 128], start=True, stop=True), "pe_set", [t, lw, free["M"]])
            add("dv", lambda e: e.tensor_scalar(gt[:, 0:CH], Mb[:, :], 0.0, 2.0, ALU.is_ge, ALU.mult), "dv_set", [tm])
            gf = gB[:, :, :].rearrange("p g n -> p (g n)")
            t2 = add("dv", lambda e: e.tensor_copy(gf, Mb[:, :]), "dv_set")
            free["M"] = t2
            t2 = add("dv", lambda e: e.scalar_tensor_tensor(gt[:, CH:], gf, -1.0, gf, ALU.mult, ALU.max), "dv_set", [t2])
            t2 = add("dv", lambda e: e.tensor_scalar(gt[:, CH:], gt[:, CH:], 0.25, None, ALU.max), "dv_set", [t2])
            return add("dv", lambda e: e.scalar_tensor_tensor(gf, gt[:, 0:CH], -1.0, gt[:, CH:], ALU.add, ALU.mult), "dv_set", [t2])

        def scale_w(w, g):
            return add("po", lambda e: e.tensor_tensor(w[:, :], w[:, :], gB[:, g, :], ALU.mult), "po_set", [tg, l1])

        xh_tok = [None, None]

        ln_tok = {}

        def ln_a(c, x_ready, xt=None):
            own = xt is None
            xh_free = xh_tok[c % 2] if own else t_zx
            if xt is None:
                xt = lambda t: xh[:, t % 8, :]
            for t_ in range(4 * c, 4 * c + 4):
                a = add("dv", lambda e, t_=t_: e.bn_stats(st[:, t_, :], xs[:, t_, :]), "dv_ln", [x_ready])
            stats = a
            for t_ in range(4 * c, 4 * c + 4):
                a = add("dv", lambda e, t_=t_: e.bn_aggr(mv[:, t_, :], st[:, t_, :]), "dv_ln", [stats])
            cs_ = slice(4 * c, 4 * c + 4)
            b = add("po", lambda e: e.tensor_scalar(ve[:, cs_], mv[:, cs_, 1], EPS, None, ALU.add), "po_ln", [a])
            b = add("po", lambda e: e.tensor_tensor(rs[:, cs_], ve[:, cs_], mh[:, :], ALU.pow), "po_ln", [b, t_mh])
            ln_tok[c] = (b, xh_free, xt, own)

        def ln_n(c):
            b, xh_free, xt, own = ln_tok[c]
            for t_ in range(4 * c, 4 * c + 4):
                d = add("dv", lambda e, t_=t_: e.tensor_scalar(xt(t_), xs[:, t_, :], mv[:, t_, 0:1], rs[:, t_:t_ + 1],
                                                               ALU.subtract, ALU.mult), "dv_xh", [b, xh_free])
            ln_tok[c] = (d, xt, own)

        def ln_b(c, layer, second, bank, bkey, hT_free):
            d, xt, own = ln_tok[c]
            k = 2 if second else 0
            for j in range(4):
                p = add("pe", lambda e, j=j: e.transpose(bank[:, 128 * j:128 * j + 128], xt(4 * c + j), idf[:, :]),
                        "pe_ln", [d, free[bkey], t_id])
            f = add("ac", lambda e: e.activation(hT[:, 1 + CH * c:1 + CH * c + CH], bank, ACT.Identity,
                                                 bias=mc[:, layer, k:k + 1], scale=mc[:, layer, k + 1:k + 2]),
                    "ac_h", [p, hT_free, tmc[layer, k]])
            free[bkey] = f
            if own:
                xh_tok[c % 2] = p
            return f, p

        def hc(c, a=0, b=CH):
            return hT[:, 1 + CH * c + a:1 + CH * c + b]

        split_state = {"n": 0, "wr": [[] for _ in range(5)]}

        def split(bank, bkey, ready, rows, bias, scale, place, sub="po", defer=False):
            n = split_state["n"]
            split_state["n"] += 1
            s = n if n < 3 else 3 + n % 2
            prev = split_state["wr"][s]
            f = (qf[0:rows, n % 2, :], (PT[0][:, 0:CH], PT[0][:, CH:], Os[:, 0, :])[n % 3][0:rows])[n < 3]
            parts = (q3[0:rows, n % 2, :, :],
                     PT[1 + n % 3][0:rows, 0:768].bitcast(BF16).rearrange("p (s n) -> p s n", s=3))[n < 3]
            if bias is None:
                a = add("ac", lambda e: e.activation(f, bank[0:rows, :], ACT.Copy, scale=scale), "ac_sp", [ready] + prev)
            else:
                a = add("ac", lambda e: e.activation(f, bank[0:rows, :], ACT.Identity, bias=bias, scale=scale), "ac_sp",
                        [ready, tbq] + prev)
            free[bkey] = a
            p = [parts[:, i, :] for i in range(3)]
            split_state["wr"][s] = []
            b = add("ac", lambda e: e.activation(p[0], f, ACT.Copy), "ac_sp", [a])

            def rest():
                r = add(sub, lambda e: e.tensor_tensor(f, f, p[0], ALU.subtract), sub + "_sp", [b])
                d = add(sub, lambda e: e.tensor_copy(p[1], f), sub + "_sp", [r])
                g = add(sub, lambda e: e.tensor_tensor(p[2], f, p[1], ALU.subtract), sub + "_sp", [d])
                split_state["wr"][s] = place(parts, g)
                return split_state["wr"][s]
            return rest if defer else rest()

        RUNS = {"q": ((0, 3, 0), (3, 2, 1), (5, 1, 2)), "k": ((0, 3, 0), (3, 2, 0), (5, 1, 0))}

        def store_rows(kind, scr, parts, sig, tok):
            rows, _, n = parts.shape
            for j, k, p0 in RUNS[kind]:
                src = parts[:, p0:p0 + k, :] if kind == "k" else parts[:, p0:p0 + 1, :].to_broadcast([rows, k, n])
                t = dma(scr[j:j + k].rearrange("s p n -> p s n"), src, sig, [tok])
            return t

        t_q, t_k, t_v, hts = [], [], [], []

        def slab0(which, c, parts, tok):
            cols = slice(CH * c, CH * c + CH) if which == "k" else slice(CH * (c % 2), CH * (c % 2) + CH)
            scr = scratch[which][:, :, CH * c:CH * c + CH]
            tw = store_rows(which, scr, parts, f"sw{which}{c}", tok)

            def load():
                for par in range(2):
                    slab = Ks[48 * par:48 * par + 48, :, cols] if which == "k" else Qs[48 * par:48 * par + 48, par:16:2, cols]
                    done = dma(slab, scr.rearrange("j (d two h) n -> two (j d) h n", two=2, h=8)[par], f"sl{which}{c}",
                               [tw] + ([t_qz[c % 2]] + q_free.get(c, []) if which == "q" else []))
                (t_k if which == "k" else t_q).append(done)
            loads.append(load)
            return [tw]

        loads = []

        def load_slabs(keep=0):
            while len(loads) > keep:
                loads.pop(0)()

        q_free = {}

        def project_k(c, bank, key):
            p = add("pe", lambda e: e.matmul(bank[:, :], wkT[:, :], hc(c), start=True, stop=True), "pe_pr", [hts[c][0], free[key], l0])
            rest = split(bank, key, p, 128, bk[:, :], 1.0, lambda parts, g: slab0("k", c, parts, g), "dv", defer=True)
            return rest

        def project_q(c, bank=Mb, key="M", sub="po", defer=False):
            p = add("pe", lambda e: e.matmul(bank[:, :], wqT[:, :], hc(c), start=True, stop=True), "pe_pr", [hts[c][0], free[key], l0])
            rest = split(bank, key, p, 128, bqs[:, :], 8.0 ** -0.5, lambda parts, g: slab0("q", c, parts, g), sub, defer=True)
            if defer:
                return rest
            rest()
            load_slabs()

        def project_v(c):
            bank, key = ((Ob, "O"), (Mb, "M"))[c % 2]
            for j in range(4):
                p = add("pe", lambda e, j=j: e.matmul(bank[:, 128 * j:128 * j + 128], hc(c, 128 * j, 128 * j + 128), wvT[:, :],
                                                      start=True, stop=True), "pe_pr", [free[key], hts[c][0], lv])
            for j in range(4):
                t = add("dv", lambda e, j=j: e.tensor_tensor(
                    Va[:, 4 * c + j, :, 0:8], bank[:, 128 * j:128 * j + 128].rearrange("p (h d) -> p h d", d=8),
                    bvB[:, :].rearrange("p (h d) -> p h d", d=8), ALU.add), "dv_v", [p, t_va[c], lv])
            free[key] = t
            t_v.append(t)

        def turn0(c):
            hts.append(ln_b(c, 0, False, At[c % 2][:, 0:CH], f"A{c % 2}", None))

        def output_bias0(c):
            return add("po", lambda e: e.tensor_tensor(xs[:, 4 * c:4 * c + 4, :], xs[:, 4 * c:4 * c + 4, :],
                       boB[:, :].unsqueeze(1).to_broadcast([128, 4, 128]), ALU.add), "po_xb", [hts[c][1], R["dn"]])

        def attention(L, units, smm, stmm, vmm, width, dcols, d_ready, shift_dst, wout, t_wout, x_ready, s_ready, st_ready,
                      before=(), hooks=(), on_chunk=None):
            nU = len(units)
            steps = [(u, kt) for u in range(nU) for kt in range(width(u, None))]
            stiles = []
            for u in range(nU):
                stiles += [(u,) + x for x in smm(u, None)]
            n_of = [width(u, None) for u in range(nU)]
            state = {"si": 0, "b": 2, "hook": None}
            now = [-2]
            later = {}
            urgent = []
            shift = [None] * nU
            x_done = {}

            def at(step, fn):
                later.setdefault(step, []).append(fn)

            def emit_s(J):
                i = state["si"]
                if i >= len(stiles):
                    return
                state["si"] += 1
                u, qt, h4, kb, mms = stiles[i]
                state["b"] = (state["b"] + 1) % 3
                if state["b"] == 2 and J >= 0 and (state["hook"] == now[0] or any(k <= now[0] + 1 for k in later) or (urgent and urgent[0][0] <= now[0] + 1)):
                    state["b"] = 0
                key, bank = (("S0", Sb[0]), ("S1", Sb[1]), ("M", Mb))[state["b"]]
                for m, (o, lt, rh, start, stop) in enumerate(mms):
                    p = add("pe", lambda e, o=o, lt=lt, rh=rh, start=start, stop=stop: e.matmul(
                        bank[:, o[0]:o[1]], lt, rh, start=start, stop=stop, skip_group_check=not start),
                        f"at_S", [free[key]] + (s_ready(u, kb) if m == 0 else []))
                n = max(o[1] for o, *_ in mms)
                t_mx = free[key] = add("dv", lambda e: e.tensor_reduce(mx[:, u, 4 * qt + h4, kb:kb + 1], bank[:, 0:n], AX.X, ALU.max),
                               f"at_mx", [p])
                last = i + 1 == len(stiles) or stiles[i + 1][0] != u
                if last:
                    nk = max(x[3] for x in stiles if x[0] == u) + 1
                    a = add("dv", lambda e: e.tensor_reduce(nm[:, u, :], mx[:, u, :, 0:nk], AX.X, ALU.max, negate=True),
                            f"at_nm", [t_mx])
                    nv = nm[:, u, :]
                    rv = nr[:, u, :]
                    z = n3[:, u, :, :, :].rearrange("p q h s -> p (q h) s")
                    a = add("po", lambda e: e.tensor_copy(z[:, :, 0], nv), f"at_n3", [a])
                    a = add("po", lambda e: e.tensor_tensor(rv, nv, z[:, :, 0], ALU.subtract), f"at_n3", [a])
                    a = add("po", lambda e: e.tensor_copy(z[:, :, 1], rv), f"at_n3", [a])
                    t_n3 = add("po", lambda e: e.tensor_tensor(z[:, :, 2], rv, z[:, :, 1], ALU.subtract), f"at_n3", [a])

                    def turn():
                        Mh = Mb[:, :].bitcast(BF16)
                        for qt_ in range(4):
                            p = add("pe", lambda e, qt_=qt_: e.transpose(Mh[0:12, 128 * qt_:128 * qt_ + 128],
                                    n3[:, u, qt_, :, :].rearrange("p h s -> p (h s)"), idb[:, :]),
                                    f"at_mT", [t_n3, free["M"], t_idb])
                        a = add("ac", lambda e: e.activation(nrow[:, u % 2, :], Mh[0:12, 0:CH], ACT.Copy), f"at_nr",
                                [p, shift[u - 2] if u >= 2 else shift0[u % 2]])
                        free["M"] = a
                        for h4_ in range(4):
                            shift[u] = dma(shift_dst(u, h4_), nrow[3 * h4_:3 * h4_ + 3, u % 2, :], f"at_sh{u % 4}", [a])
                    urgent.append((J + 2, turn))

            shift0 = attention.shift_last
            pv_tok = {}
            ex_tok = {}

            def emit_st(j, pair):
                u, kt = steps[j]
                assert shift[u] is not None
                lo, mms = stmm(u, kt, pair)
                for m, (o, lt, rh, start, stop) in enumerate(mms):
                    p = add("pe", lambda e, o=o, lt=lt, rh=rh, start=start, stop=stop: e.matmul(
                        At[pair][:, o[0]:o[1]], lt, rh, start=start, stop=stop, skip_group_check=not start),
                        f"at_T", [free[f"A{pair}"], shift[u]] + (st_ready(u) if m == 0 else []))
                slot = (2 * j + pair) % 4
                ai = At[pair][:, :].rearrange("p (i n) -> p i n", i=2)[:, :, lo:CH]
                ao = PT[slot][:, :].rearrange("p (i n) -> p i n", i=2)[:, :, lo:CH]
                t = add("ac", lambda e: e.activation(ao, ai, ACT.Exp), f"at_ex", [p, pv_tok.get((j - 2, pair))])
                free[f"A{pair}"] = t
                ex_tok[(j, pair)] = t

            def emit_pv(j, pair):
                if j < 0:
                    return
                u, kt = steps[j]
                lo = width(u, kt)
                slot = (2 * j + pair) % 4
                for i in range(2):
                    g = 2 * pair + i
                    p = add("pe", lambda e, g=g, i=i: e.matmul(Ob[32 * g:32 * g + 32, lo:CH], vmm(u, kt, g),
                            PT[slot][:, CH * i + lo:CH * i + CH], start=(kt == 0), stop=True,
                            skip_group_check=(kt > 0), tile_position=(0, 32 * g)), f"at_pv", [ex_tok[(j, pair)], free["O"], d_ready(u, kt)])
                pv_tok[(j, pair)] = p
                if kt == n_of[u] - 1 and pair == 1:
                    finish(u, j, p)

            def finish(u, j, p):
                c, quad = units[u]
                p_last = p
                prev = os_tok[u % 2]
                o = add("ac", lambda e: e.activation(Os[:, u % 2, :], Ob[:, :], ACT.Copy), f"at_os", [p, prev])
                free["O"] = o

                def turn():
                    for qt in range(4):
                        p = add("pe", lambda e, qt=qt: e.transpose(Mb[:, 128 * qt:128 * qt + 128],
                                Os[:, u % 2, 128 * qt:128 * qt + 128], idf[:, :]), f"at_oT", [o, free["M"]])
                    os_tok[u % 2] = p
                    Mq = Mb[:, :].rearrange("p (x w) -> p x w", w=32)
                    r = add("dv", lambda e: e.reciprocal(rl[:, u, :], Mq[:, :, dcols]), f"at_rl", [p])
                    nq = 128 // (4 * dcols)
                    for qt in range(4):
                        w = add("dv", lambda e, qt=qt: e.tensor_tensor(
                            vw[:, c % 2, qt, 4 * dcols * quad:4 * dcols * quad + 4 * dcols].rearrange("p (g d) -> p g d", d=dcols),
                            Mq[:, 4 * qt:4 * qt + 4, 0:dcols],
                            rl[:, u, 4 * qt:4 * qt + 4].unsqueeze(2).to_broadcast([128, 4, dcols]), ALU.mult),
                            f"at_vw", [r, vw_tok[c % 2]])
                    free["M"] = w
                    if quad == nq - 1:
                        def back():
                            for qt in range(4):
                                p = add("pe", lambda e, qt=qt: e.transpose(Mb[:, 128 * qt:128 * qt + 128],
                                        vw[:, c % 2, qt, :], idf[:, :]), f"at_wT", [w, free["M"]])
                            vw_tok[c % 2] = p
                            a = add("ac", lambda e: e.activation(vwT[:, c % 2, :], Mb[:, :], ACT.Copy), f"at_wc",
                                    [p, y_tok[c % 2]])
                            free["M"] = a
                            at(now[0] + 1, lambda: project(a))

                        def project(a):
                            for qt in range(4):
                                p = add("pe", lambda e, qt=qt: e.matmul(Mb[:, 128 * qt:128 * qt + 128],
                                        vwT[:, c % 2, 128 * qt:128 * qt + 128], wout[:, :], start=True, stop=True),
                                        f"at_y", [a, R[t_wout], free["M"]])
                            y_tok[c % 2] = p
                            xv = xs[:, 4 * c:4 * c + 4, :]
                            x = add("dv", lambda e: e.tensor_tensor(xv, xv, Mb[:, :].rearrange("p (t n) -> p t n", t=4), ALU.add),
                                    f"at_x", [p, ("po_xb", counts["po_xb"])])
                            free["M"] = x
                            x_done[c] = x
                            if on_chunk:
                                on_chunk(c, x, p_last, at, now[0])
                        at(now[0] + 1, back)
                at(now[0] + 2, turn)

            os_tok, vw_tok, y_tok = attention.os_tok, attention.vw_tok, attention.y_tok
            for J0, fn in hooks:
                at(J0, fn)

            def do_later(one=True):
                while True:
                    ks = [k for k in later if k <= now[0]]
                    if urgent and urgent[0][0] <= now[0]:
                        fn = urgent.pop(0)[1]
                    elif ks:
                        k = min(ks)
                        fn = later[k].pop(0)
                        if not later[k]:
                            later.pop(k)
                    else:
                        break
                    state["hook"] = now[0]
                    fn()
                    if one:
                        break

            starts = [sum(n_of[:u]) for u in range(nU)]
            of_unit = [len([1 for x in stiles if x[0] == u]) for u in range(nU)]

            def due(j):
                return sum(n for n, s0_ in zip(of_unit, starts) if s0_ - LEAD <= j)

            for J in range(len(steps) + 1):
                now[0] = J
                if J == 0:
                    first = len([1 for x in stiles if x[0] == 0])
                    for fn in before:
                        if callable(fn):
                            fn()
                        else:
                            for _ in range(fn):
                                emit_s(-2)
                    while state["si"] < first:
                        emit_s(-2)
                k = 0
                for j2 in range(J, len(steps)):
                    k = max(k, -(-(due(j2) - state["si"]) // (j2 - J + 1)))
                do_later()
                order = (1, 3, 0, 4, 2)
                parts = [k // 5 + (1 if order.index(i) < k % 5 else 0) for i in range(5)]
                def s_part(i):
                    for _ in range(parts[i]):
                        emit_s(J)
                s_part(0)
                if J < len(steps):
                    emit_st(J, 0)
                do_later()
                s_part(1)
                emit_pv(J - 1, 0)
                s_part(2)
                emit_pv(J - 1, 1)
                s_part(3)
                if J < len(steps):
                    emit_st(J, 1)
                s_part(4)
            while later:
                now[0] += 1
                do_later(False)
            attention.shift_last = [shift[nU - 2], shift[nU - 1]] if nU % 2 == 0 else [shift[nU - 1], shift[nU - 2]]
            attention.last_pv = pv_tok[(len(steps) - 1, 1)]
            attention.last_ex = [free["A0"], free["A1"]]
            return x_done

        attention.shift_last = [None, None]
        attention.os_tok, attention.vw_tok, attention.y_tok = [None, None], [None, None], [None, None]

        units0 = [(c, q) for c in range(4) for q in range(4)]

        def s0(u, _):
            c, quad = units0[u]
            r = []
            order = [(qt, kb) for kb in range(4) for qt in range(4)] if u == 0 else [(qt, kb) for qt in range(4) for kb in range(4)]
            for qt, kb in order:
                for h4 in range(4):
                    hd = 4 * quad + h4
                    q0 = CH * (c % 2) + 128 * qt
                    r.append((qt, h4, kb, [((0, CH), Qs[0:96, hd, q0:q0 + 128], Ks[0:96, hd // 2, CH * kb:CH * kb + CH], True, True)]))
            return r

        def st0(u, kt, pair):
            c, quad = units0[u]
            q0 = CH * (c % 2)
            return 0, [((CH * i, CH * i + CH), Ks[0:99, (4 * quad + 2 * pair + i) // 2, 128 * kt:128 * kt + 128],
                        Qs[0:99, 4 * quad + 2 * pair + i, q0:q0 + CH], True, True) for i in range(2)]

        def sh0(u, h4):
            c, quad = units0[u]
            return Qs[96:99, 4 * quad + h4, CH * (c % 2):CH * (c % 2) + CH]

        R = {}

        def route(c, bank, key):
            ts = slice(4 * c, 4 * c + 4)
            R[c] = ln_b(c, 0, True, bank[:, :], key, hts[c][0])
            for j in range(4):
                p = add("pe", lambda e, j=j: e.matmul(bank[:, 16 * j:16 * j + 16], hc(c, 128 * j, 128 * j + 128), rwT[:, :],
                                                      start=True, stop=True), "ff_lg", [R[c][0], free[key], l1])
            a = add("dv", lambda e: e.tensor_copy(lg, bank[:, 0:64].rearrange("p (t n) -> p t n", t=4)), "ff_r", [p])
            free[key] = a
            b4 = lambda v: v.to_broadcast([128, 4, 16])
            a = add("dv", lambda e: e.tensor_reduce(lm[:, ts], lg, AX.X, ALU.max), "ff_r", [a])
            a = add("dv", lambda e: e.tensor_tensor(eq, lg, b4(lm[:, ts].unsqueeze(2)), ALU.is_equal), "ff_r", [a])
            a = add("dv", lambda e: e.tensor_tensor(wv_, eq, b4(desc[:, :].unsqueeze(1)), ALU.mult), "ff_r", [a, R["desc"]])
            a = add("dv", lambda e: e.tensor_reduce(wm[:, :], wv_, AX.X, ALU.max), "ff_r", [a])
            a = add("dv", lambda e: e.tensor_tensor(OH[:, ts, :], wv_, b4(wm[:, :].unsqueeze(2)), ALU.is_equal), "ff_r", [a])
            R["oh"] = add("dv", lambda e: e.tensor_copy(OHb[:, ts, :], OH[:, ts, :]), "ff_r", [a])

        def next_q(c, x, p, at, now):
            if c + 2 < 4:
                q_free[c + 2] = [p]
                at(now + 1, lambda: project_q(c + 2))
            if c < 3:
                at(now + 3, lambda: ln_a(c, x, lambda t: XP[:, t, 0:128]))
                at(now + 6, lambda: ln_n(c))
                at(now + 8, lambda: route(c, Mb, "M"))

        ams = [PT[2][:, 0:CH], PT[2][:, CH:], PT[3][:, 0:CH], PT[3][:, CH:]]
        bsg, bt = (PT[i][:, :].rearrange("p (k n) -> p k n", k=2) for i in range(2))
        am_free, bt_tok, bsg_tok = [None] * 4, [None, None], [None, None]
        hfree, xd1, pend = {}, {}, []

        def shared_up(c, bl):
            k, s = bl % 2, bl % 4
            pvs = ("at_pv", counts["at_pv"])
            G, U = At[k][:, 0:CH], At[k][:, CH:]
            for W, O_ in ((sgT, G), (suT, U)):
                p = add("pe", lambda e, W=W, O_=O_: e.matmul(O_, W[:, 128 * bl:128 * bl + 128], hc(c), start=True, stop=True),
                        "ff_sh", [R[c][0], free[f"A{k}"], l1])
            a = add("ac", lambda e: e.activation(bsg[:, k, :], G, ACT.Sigmoid), "ff_sg", [p, bsg_tok[k], pvs])
            b = add("dv", lambda e: e.tensor_tensor(bt[:, k, :], G, bsg[:, k, :], ALU.mult), "ff_d", [a, bt_tok[k], pvs])
            bsg_tok[k] = b
            d = add("dv", lambda e: e.tensor_tensor(ams[s], U, bt[:, k, :], ALU.mult), "ff_d", [b, am_free[s]])
            bt_tok[k] = free[f"A{k}"] = d
            hfree[c] = p
            return s, d

        def shared_down(c, bl, s, tok):
            bank, key = ((Ob, "O"), (Sb[1], "S1"))[c % 2]
            for j in range(4):
                p = add("pe", lambda e, j=j: e.matmul(bank[:, 128 * j:128 * j + 128], ams[s][:, 128 * j:128 * j + 128], sdT[:, bl, :],
                        start=(bl == 0 and j == 0), stop=True, skip_group_check=not (bl == 0 and j == 0)), "ff_y",
                        [tok, free[key], R["dn"]])
            am_free[s] = p
            if bl == 3:
                xv = xs[:, 4 * c:4 * c + 4, :]
                x = add("dv", lambda e: e.tensor_tensor(xv, xv, bank[:, :].rearrange("p (t n) -> p t n", t=4), ALU.add), "ff_x", [p])
                free[key] = x
                xd1[c] = x

        def shared_block(c, bl):
            pend.append((c, bl) + shared_up(c, bl))
            if len(pend) > 2:
                shared_down(*pend.pop(0))

        def shared_flush():
            while pend:
                shared_down(*pend.pop(0))

        tcs = mod_silu()
        ln_a(0, lx[0])
        mod_columns([(0, 0), (0, 1)], lwa)
        tbq = add("dv", lambda e: e.tensor_scalar(bqs[:, :], bq[:, :], 8.0 ** -0.5, None, ALU.mult), "dv_set", [l0])
        ln_a(1, lx[1])
        ln_n(0)
        turn0(0)
        ln_n(1)
        k0 = project_k(0, Sb[1], "S1")
        turn0(1)
        ln_a(2, lx[2])
        q0 = project_q(0, Sb[0], "S0", "dv", defer=True)
        ln_a(3, lx[3])
        ln_n(2)
        turn0(2)
        ln_n(3)
        turn0(3)
        k0()
        k1 = project_k(1, Sb[1], "S1")
        q0()
        load_slabs(1)
        k2 = project_k(2, Sb[0], "S0")
        k1()
        load_slabs(1)
        k3 = project_k(3, Sb[1], "S1")
        k2()
        load_slabs(1)
        k3()
        load_slabs()
        for c in range(1, 4):
            t_va.append(add("po", lambda e, c=c: e.memset(Va[:, 4 * c:4 * c + 4, :, :], 1.0), "c4"))
        t_idb = add("po", lambda e: e.tensor_copy(idb[:, :], idf[:, :]), "c1", [t_id])
        t_k1 = add("po", lambda e: e.memset(Ks[96:128, :, :].bitcast(U32), 0x3F803F80), "c4", [t_idb])
        t_qz.append(add("po", lambda e: e.memset(Qs[:, :, CH:2 * CH].bitcast(F32), 0.0), "c4", [t_k1]))
        for c in range(4):
            project_v(c)
        l1 = load_rest()
        t_ub, t_zx = more_constants()

        def scaled_weights():
            nonlocal tg
            mod_columns([(0, 2), (0, 3), (1, 0), (1, 1), (1, 2), (1, 3)], lw)
            tg = gates()
            R["wo"] = scale_w(woT, 0)
            scale_w(boB, 0)
            scale_w(bpB, 2)
            R["wp"] = scale_w(wp1, 2)
            R["wvv"] = scale_w(wvv, 3)
            R["dn"] = add("po", lambda e: e.tensor_tensor(sdT[:, :, :], sdT[:, :, :], gB[:, 1, :].unsqueeze(1).to_broadcast([128, 4, 128]), ALU.mult), "po_set")
            for c in range(4):
                output_bias0(c)

        tg = None
        xd0 = attention(0, units0, s0, st0, lambda u, kt, g: Va[:, kt, 4 * units0[u][1] + g, :],
                        lambda u, kt: 16 if kt is None else 0, 8, lambda u, kt: t_v[kt // 4], sh0, woT, "wo", None,
                        lambda u, kb: [t_k[kb], t_q[units0[u][0]]],
                        lambda u: [t_k1, t_q[units0[u][0]]],
                        hooks=[(1, scaled_weights), (4, lambda: project_q(1)), (12, late_constants)] +
                              [(257 + bl, lambda bl=bl: shared_block(0, bl)) for bl in range(4)], on_chunk=next_q)
        pv0 = attention.last_pv

        Vf = Va[:, :, :, :].rearrange("p k h w -> p (k h w)")
        Kf = Ks[:, 0:6, :].rearrange("p k n -> p (k n)").bitcast(F32)
        ln_a(3, xd0[3], lambda t: XP[:, t, 0:128])
        shared_block(1, 0)
        ln_n(3)
        for bl in range(1, 4):
            shared_block(1, bl)
        route(3, Sb[0], "S0")

        p = add("pe", lambda e: e.matmul(Mb[:, 0:256], Ub[:, :], OHb[:, :, :].rearrange("p t n -> p (t n)"),
                                         start=True, stop=True), "ff_rk", [R["oh"], free["M"], t_ub])
        for t in range(15):
            p = add("pe", lambda e, t=t: e.matmul(Mb[:, 16 * t + 16:256].rearrange("p (t n) -> p t n", n=16), onesb[:, :],
                    OHb[:, t:t + 1, :].to_broadcast([128, 15 - t, 16]), start=False, stop=True, skip_group_check=True), "ff_rk")
        for t in range(16):
            p = add("pe", lambda e, t=t: e.matmul(Sb[0][:, 0:16], onesb[:, :], OHb[:, t, :], start=(t == 0), stop=(t == 15)),
                    "ff_rk", [free["S0"]])
        K0 = 3968
        def kv(n, *shape):
            nonlocal K0
            v = Kf[:, K0:K0 + n]
            K0 += n
            return v
        cmp_ = kv(256).rearrange("p (n k) -> p n k", n=16)
        tot, til, sta, end, s128 = (kv(16) for _ in range(5))
        post = kv(256).rearrange("p (t n) -> p t n", t=16)
        cm2 = kv(16 * NT).rearrange("p (i n) -> p i n", i=NT)
        posf, ef = kv(16), kv(NT)
        sq = lambda v: v.to_broadcast([128, 16, 16])
        a = add("dv", lambda e: e.tensor_copy(tot, Sb[0][:, 0:16]), "ff_p", [p, R["it"]])
        free["S0"] = a
        a = add("dv", lambda e: e.tensor_tensor(cmp_, sq(tot.unsqueeze(2)), sq(k128[:, :].unsqueeze(1)), ALU.is_gt), "ff_p", [a])
        a = add("dv", lambda e: e.tensor_reduce(til, cmp_, AX.X, ALU.add), "ff_p", [a])
        a = add("dv", lambda e: e.tensor_tensor(cmp_, LT[:, :, :], sq(til.unsqueeze(1)), ALU.mult), "ff_p", [a])
        a = add("dv", lambda e: e.tensor_reduce(sta, cmp_, AX.X, ALU.add), "ff_p", [a])
        add("dv", lambda e: e.tensor_tensor(end, sta, til, ALU.add), "ff_p", [a])
        a = add("dv", lambda e: e.tensor_scalar(s128, sta, 128.0, None, ALU.mult), "ff_p")
        t_end = a
        a = add("dv", lambda e: e.tensor_tensor(post, Mb[:, 0:256].rearrange("p (t n) -> p t n", t=16), sq(s128.unsqueeze(1)),
                                                ALU.add), "ff_p", [a])
        free["M"] = a
        a = add("dv", lambda e: e.tensor_tensor(post, post, OH[:, :, :], ALU.mult), "ff_p", [a])
        a = add("dv", lambda e: e.tensor_reduce(posf, post, AX.X, ALU.add), "ff_p", [a])
        t_pos = add("dv", lambda e: e.tensor_copy(posu[:, :], posf), "ff_p", [a])
        t_sc = add("ac", lambda e: e.activation(XP[:, :, 128], lm[:, :], ACT.Sigmoid), "ff_sc", [R["oh"], t_zx])
        a = add("dv", lambda e: e.tensor_tensor(cm2, end.unsqueeze(1).to_broadcast([128, NT, 16]),
                                                itf[:, 0:NT].unsqueeze(2).to_broadcast([128, NT, 16]), ALU.is_le), "ff_p", [t_end])
        a = add("dv", lambda e: e.tensor_reduce(ef, cm2, AX.X, ALU.add), "ff_p", [a])
        a = add("dv", lambda e: e.tensor_scalar(ef, ef, 15.0, 128.0, ALU.min, ALU.mult), "ff_p", [a])
        a = add("dv", lambda e: e.tensor_scalar(ef, ef, itf[:, 32:33], None, ALU.add), "ff_p", [a])
        t_idx = add("dv", lambda e: e.tensor_copy(idxu[:, :], ef), "ff_p", [a])
        off = lambda v: bass.IndirectOffsetOnAxis(ap=v, axis=0)
        for t in range(16):
            t_sx = add("po", lambda e, t=t: e.indirect_dma_start(out=sorted_x, out_offset=off(posu[:, t:t + 1]),
                       in_=XP[:, t, :], in_offset=None), "sx", [t_pos, t_sc, R[3][1], t_zx], by=16)

        XS = Vf[:, 0:NT * PW].rearrange("p (i n) -> p i n", i=NT)
        NW = 16
        Qf = Qs[:, :, :].rearrange("p h n -> p (h n)").bitcast(F32)
        Wt = [Qf[:, 384 * i:384 * i + 384] for i in range(NW)]
        ring = lambda k: [Vf[:, 5920 + 512 * k + 128 * i:5920 + 512 * k + 128 * i + 128] for i in range(4)]
        hS, sgS, acS, aT = (ring(k) for k in range(4))
        YS = Kf[:, 0:NT * 128].rearrange("p (i n) -> p i n", i=NT)
        wall = A["L0_ffn_experts"]
        wtok, wfree = {}, {}

        def fetch_w(i):
            wtok[i] = add("po", lambda e: e.indirect_dma_start(out=Wt[i % NW], out_offset=None, in_=wall,
                          in_offset=off(idxu[:, i:i + 1])), f"wt{i % NW}", [t_idx, pv0, wfree.get(i - NW)], by=16)

        for i in range(NW):
            fetch_w(i)
        xtok = {}
        for b_ in range(0, NT, 4):
            e_ = min(b_ + 4, NT)
            t = dma(XS[:, b_:e_, :], sorted_x.rearrange("(i p) n -> p i n", p=128)[:, b_:e_, :], f"xs{b_}", [t_sx, pv0])
            for i in range(b_, e_):
                xtok[i] = t

        for bl in range(4):
            shared_block(2, bl)
        shared_flush()

        banks = {"t1": [At[0][:, 0:128], At[0][:, CH:CH + 128]], "gu": [At[1][:, 0:256], At[1][:, CH:CH + 256]],
                 "t2": [Sb[0][:, 0:128], Sb[1][:, 0:128]], "y": [Ob[:, 0:128], Mb[:, 0:128]]}
        bf = {"t1": [free["A0"]] * 2, "gu": [free["A1"]] * 2, "t2": [free["S0"], free["S1"]], "y": [free["O"], free["M"]]}
        hs_t, gu_t, a_t, at_t, rf = {}, {}, {}, {}, {}

        def st_t1(i):
            k = i % 2
            p = add("pe", lambda e: e.transpose(banks["t1"][k], XS[:, i, 0:128], idf[:, :]), "m_t1", [xtok[i], bf["t1"][k]])
            bf["t1"][k] = hs_t[i] = add("ac", lambda e: e.activation(hS[i % 4], banks["t1"][k], ACT.Identity,
                bias=mc[:, 0, 2:3], scale=mc[:, 0, 3:4]), "m_h", [p, gu_t.get(i - 4), pv0])

        def st_gu(i):
            k = i % 2
            gu_t[i] = p = add("pe", lambda e: e.matmul(banks["gu"][k], hS[i % 4], Wt[i % NW][:, 0:256], start=True, stop=True),
                              "m_gu", [hs_t[i], wtok[i], bf["gu"][k]])
            G, U, sc = banks["gu"][k][:, 0:128], banks["gu"][k][:, 128:256], XS[:, i, 128:129]
            a = add("ac", lambda e: e.activation(sgS[i % 4], G, ACT.Sigmoid, scale=sc), "m_sg", [p, rf.get((i - 4, "sg"))])
            b = add("dv", lambda e: e.scalar_tensor_tensor(sgS[i % 4], G, sc, sgS[i % 4], ALU.mult, ALU.mult), "m_d", [a])
            d = add("dv", lambda e: e.scalar_tensor_tensor(acS[i % 4], U, sc, sgS[i % 4], ALU.mult, ALU.mult), "m_d",
                    [b, rf.get((i - 4, "a"))])
            rf[i, "sg"] = d
            bf["gu"][k] = a_t[i] = d

        def st_t2(i):
            k = i % 2
            p = add("pe", lambda e: e.transpose(banks["t2"][k], acS[i % 4], idf[:, :]), "m_t2", [a_t[i], bf["t2"][k]])
            rf[i, "a"] = p
            bf["t2"][k] = at_t[i] = add("dv", lambda e: e.tensor_copy(aT[i % 4], banks["t2"][k]), "m_c", [p, rf.get((i - 4, "y"))])

        def st_y(i):
            k = i % 2
            p = add("pe", lambda e: e.matmul(banks["y"][k], aT[i % 4], Wt[i % NW][:, 256:384], start=True, stop=True), "m_y",
                    [at_t[i], bf["y"][k]])
            rf[i, "y"] = wfree[i] = p
            y = add("dv", lambda e: e.tensor_tensor(YS[:, i, :], banks["y"][k], gB[:, 1, :], ALU.mult), "m_ys", [p])
            bf["y"][k] = y
            if i % 4 == 3 or i == NT - 1:
                b_ = i // 4 * 4
                R["yd"] = dma(sorted_y.rearrange("(i p) n -> p i n", p=128)[:, b_:i + 1, :], YS[:, b_:i + 1, :], "yd", [y])
            if i + NW < NT:
                fetch_w(i + NW)

        for i in range(NT + 6):
            if i < NT:
                st_t1(i)
            for lag, fn in ((2, st_gu), (4, st_t2), (6, st_y)):
                if 0 <= i - lag < NT:
                    fn(i - lag)
        free["A0"], free["A1"] = bf["t1"][(NT - 1) % 2], bf["gu"][(NT - 1) % 2]
        free["S0"], free["S1"] = bf["t2"]
        free["O"], free["M"] = bf["y"]
        for bl in range(4):
            shared_block(3, bl)
        shared_flush()
        g_tok = {}

        def gather(c):
            for t in range(4 * c, 4 * c + 4):
                g_tok[c] = add("po", lambda e, t=t: e.indirect_dma_start(out=XP[:, t, 0:128], out_offset=None, in_=sorted_y,
                               in_offset=off(posu[:, t:t + 1])), f"yg{c}", [R["yd"], t_sx], by=16)

        def accept(c):
            xv = xs[:, 4 * c:4 * c + 4, :]
            xd1[c] = add("dv", lambda e: e.tensor_tensor(xv, xv, XP[:, 4 * c:4 * c + 4, 0:128], ALU.add), "ff_x", [g_tok[c], xd1[c]])
            ln_a(c, xd1[c])

        F = {"down": hfree}

        t_q1, t_kk, t_v1s, h1 = [], [], [], []

        def setup1a(c, bank, key):
            h1.append(ln_b(c, 1, False, bank, key, F["down"][c]))
            add("po", lambda e: e.tensor_tensor(xs[:, 4 * c:4 * c + 4, :], xs[:, 4 * c:4 * c + 4, :],
                bpB[:, :].unsqueeze(1).to_broadcast([128, 4, 128]), ALU.add), "po_xb", [h1[c][1]])

        def setup1b(c, bank, key, sub="po", bank2=None, key2=None, defer=False):
            if bank2 is None:
                bank2, key2 = bank, key
            h = h1[c][0]
            cols = slice(CH * c, CH * c + CH)

            def place_k(parts, g):
                scr = scratch["k1"][:, :, cols]
                tw = store_rows("k", scr, parts, f"k1w{c}", g)
                loads.append(lambda: t_kk.append(dma(Ks[0:96, 7, cols], scr.rearrange("j d n -> (j d) n"), f"k1{c}", [tw, pv0])))
                return [tw]

            def place_q(parts, g):
                scr = scratch["q1"][:, :, cols]
                tw = store_rows("q", scr, parts, f"q1w{c}", g)
                loads.append(lambda: t_q1.append(dma(Q1[0:96, :, cols], scr.rearrange("j (d h) n -> (j d) h n", h=8), f"q1{c}", [tw, pv0])))
                return [tw]

            p = add("pe", lambda e: e.matmul(bank[0:16, :], wk1[:, :], hc(c), start=True, stop=True), "pe_p1", [h, free[key]])
            rk = split(bank, key, p, 16, None, 1.0, place_k, sub, defer)
            p = add("pe", lambda e: e.matmul(bank2[:, :], wq1[:, :], hc(c), start=True, stop=True), "pe_p1", [free[key2]])
            rq = split(bank2, key2, p, 128, None, 128.0 ** -0.5, place_q, sub, defer)
            for j in range(4):
                p = add("pe", lambda e, j=j: e.matmul(bank[:, 128 * j:128 * j + 16], hc(c, 128 * j, 128 * j + 128), wv1[:, :],
                                                      start=True, stop=True), "pe_p1", [free[key]])

            def rest():
                if defer:
                    rk()
                    rq()
                load_slabs()
                free[key] = t = add("dv", lambda e: e.tensor_copy(V1[:, 4 * c:4 * c + 4, 0:16],
                                    bank[:, :].rearrange("p (t n) -> p t n", t=4)[:, :, 0:16]), "dv_v", [p, R["v1"]])
                t_v1s.append(t)
            return rest if defer else rest()

        units1 = [(c, q) for c in range(4) for q in range(2)]

        def s1(u, _):
            c, quad = units1[u]
            r = []
            for qt in range(4):
                for kb in range(c + 1):
                    for h4 in range(4):
                        qap = Q1[0:96, 4 * quad + h4, CH * c + 128 * qt:CH * c + 128 * qt + 128]
                        n = CH if kb < c else 128 * (qt + 1)
                        m = [((0, n), qap, Ks[0:96, 7, CH * kb:CH * kb + n], True, True)]
                        if kb == c:
                            m.append(((n - 128, n), idb[:, :], mq[:, :], False, True))
                        r.append((qt, h4, kb, m))
            return r

        def st1(u, kt, pair):
            c, quad = units1[u]
            lo = width1(u, kt)
            diag = kt >= 4 * c
            r = []
            for i in range(2):
                hd = 4 * quad + 2 * pair + i
                r.append(((CH * i + lo, CH * i + CH), Ks[0:99, 7, 128 * kt:128 * kt + 128],
                          Q1[0:99, hd, CH * c + lo:CH * c + CH], True, True))
                if diag:
                    r.append(((CH * i + lo, CH * i + lo + 128), idb[:, :], mk[:, :], False, True))
            return lo, r

        def width1(u, kt):
            c = units1[u][0]
            if kt is None:
                return 4 * (c + 1)
            return max(0, 128 * (kt - 4 * c))

        mixed = {}
        mt = Vf[:, 3072:3072 + 10 * CH].rearrange("p (a n) -> p a n", n=CH)

        def mix_start(c, x, p, at, now):
            s = 5 * (c % 2)
            xr, xk, kr, sr, vv = (mt[:, s + i, :] for i in range(5))
            hp = hT[:, CH * c:CH * c + CH]
            old = mixed.get(c - 2)

            def a0():
                mixed[c, "h"] = ln_b(c, 1, True, Mb[:, :], "M", h1[c][0])

            def a1():
                h = mixed[c, "h"][0]
                hb = mixed[max(c - 1, 0), "h"][0]
                a = add("ac", lambda e: e.activation(xk, hc(c), ACT.Copy, scale=muk[:, 0:1]), "cm_a", [h, hb, old, R["om"], t_one])
                a2_ = add("ac", lambda e: e.activation(xr, hc(c), ACT.Copy, scale=mur[:, 0:1]), "cm_a")
                d = add("dv", lambda e: e.scalar_tensor_tensor(xk, hp, omk[:, 0:1], xk, ALU.mult, ALU.add), "cm_d", [a])
                d2 = add("dv", lambda e: e.scalar_tensor_tensor(xr, hp, omr[:, 0:1], xr, ALU.mult, ALU.add), "cm_d", [a2_])
                mixed[c, "xk"] = d
                mixed[c, "d"] = d2

            B2, K2 = (Sb[0], "S0") if c == 3 else (Mb, "M")
            B3, K3 = (Sb[1], "S1") if c == 3 else (Mb, "M")

            def a1b():
                p = add("pe", lambda e: e.matmul(Mb[:, :], wkk[:, :], xk, start=True, stop=True), "cm_p", [mixed[c, "xk"], free["M"]])
                a = add("ac", lambda e: e.activation(kr, Mb[:, :], ACT.Relu), "cm_a", [p])
                free["M"] = a
                eng = "dv" if c == 3 else "po"
                mixed[c, "k"] = add(eng, lambda e: e.tensor_tensor(kr, kr, kr, ALU.mult), "cm_" + eng, [a])

            def a2():
                for j in range(4):
                    p = add("pe", lambda e, j=j: e.matmul(B2[:, 128 * j:128 * j + 128], xr[:, 128 * j:128 * j + 128], wr[:, :],
                                                          start=True, stop=True), "cm_p", [mixed[c, "d"], free[K2]])
                free[K2] = mixed[c, "s"] = add("ac", lambda e: e.activation(sr, B2[:, :], ACT.Sigmoid), "cm_a", [p])

            def a3():
                for j in range(4):
                    p = add("pe", lambda e, j=j: e.matmul(B3[:, 128 * j:128 * j + 128], kr[:, 128 * j:128 * j + 128], wvv[:, :],
                                                          start=True, stop=True), "cm_p", [mixed[c, "k"], free[K3], R["wvv"]])
                a = add("dv", lambda e: e.tensor_tensor(vv, sr, B3[:, :], ALU.mult), "cm_d", [p, mixed[c, "s"]])
                free[K3] = a
                mixed[c] = a
                xv = xs[:, 4 * c:4 * c + 4, :]
                eng = "dv" if c == 3 else "po"
                a = add(eng, lambda e: e.tensor_tensor(xv, xv, vv.rearrange("p (t n) -> p t n", t=4), ALU.add), "cm_" + eng,
                        [a, mixed[c, "h"][1]])
                mixed["out"] = dma(out.rearrange("a (t p) n -> p (a t) n", p=128)[:, 4 * c:4 * c + 4, :], xv, "st_out", [a])

            for k, fn in ((1, lambda: ln_a(c, x)), (4, lambda: ln_n(c)), (6, a0), (7, a1), (9, a1b), (10, a2), (12, a3)):
                at(now + k, fn)

        gather(0)
        gather(1)
        accept(0)
        gather(2)
        ln_n(0)
        setup1a(0, Sb[0][:, :], "S0")
        rest0 = setup1b(0, Mb, "M", "dv", Ob, "O", True)
        accept(1)
        gather(3)
        rest0()
        ln_n(1)
        setup1a(1, Sb[1][:, :], "S1")
        rest0 = setup1b(1, Mb, "M", "dv", Ob, "O", True)
        accept(2)
        rest0()
        ln_n(2)
        accept(3)
        attention(1, units1, s1, st1, lambda u, kt, g: V1[:, kt, :], width1, 16, lambda u, kt: t_v1s[kt // 4],
                  lambda u, h4: Q1[96:99, 4 * units1[u][1] + h4, CH * units1[u][0]:CH * units1[u][0] + CH],
                  wp1, "wp", None,
                  lambda u, kb: [t_kk[kb], t_q1[units1[u][0]]],
                  lambda u: [t_k1, t_q1[units1[u][0]]] + t_kk[0:units1[u][0] + 1],
                  hooks=[(0, lambda: setup1a(2, Mb[:, :], "M")), (2, lambda: setup1b(2, Mb, "M")), (12, lambda: ln_n(3)),
                         (14, lambda: setup1a(3, Mb[:, :], "M")), (15, lambda: setup1b(3, Mb, "M"))],
                  on_chunk=mix_start)
        t_out = mixed["out"]
        queues["sp"].append((None, None, 0, [t_out]))

        block = ctx.enter_context(nc.Block())

        @block.sync
        def _(e):
            tail = queues["sp"].pop()
            run("sp", e)
            for s, v in tail[3]:
                e.wait_ge(sems[s], v)

        @block.tensor
        def _(e):
            run("pe", e)

        @block.vector
        def _(e):
            run("dv", e)

        @block.scalar
        def _(e):
            run("ac", e)

        @block.gpsimd
        def _(e):
            run("po", e)


_TURNED = ('L0_attn_Wq', 'L0_attn_Wk', 'L0_attn_Wv', 'L0_attn_Wo', 'L0_ffn_router_w', 'L0_ffn_shared_gate_w',
           'L0_ffn_shared_up_w', 'L0_ffn_shared_down_w', 'L1_ffn_W_r', 'L1_ffn_W_k', 'L1_ffn_W_v')


def kernel(**inputs):
    import numpy as _np
    import concourse.bacc as _bacc
    from concourse import mybir as _mybir
    from concourse.bass_utils import run_bass_kernel_spmd as _run

    nc = _bacc.Bacc("TRN2", target_bir_lowering=False, num_devices=1)
    arrays, args = {}, {}
    given = {name: _np.asarray(inputs[name]) for name in inputs}
    given['L0_ffn_experts'] = _np.concatenate([given.pop('L0_ffn_gate_up_proj').reshape(2048, 256),
                                               given.pop('L0_ffn_down_proj').reshape(2048, 128)], axis=1)
    for name in given:
        a = given[name]
        if name in ('L0_attn_Wq', 'L0_attn_Wk', 'L0_attn_bq', 'L0_attn_bk'):
            a = a.reshape(8, 2, 8, -1).transpose(2, 1, 0, 3).reshape(a.shape)
        if name == 'L1_attn_Wq':
            a = a.transpose(1, 2, 0)
        a = _np.ascontiguousarray(a.T if name in _TURNED else a)
        arrays[f"in_{name}"] = a
        args[name] = nc.dram_tensor(f"in_{name}", a.shape, _mybir.dt.from_np(a.dtype), kind="ExternalInput").ap()
    o = nc.dram_tensor("out_0", (1, 2048, 128), _mybir.dt.float32, kind="ExternalOutput").ap()
    adaln_two_layers(nc, args, o)
    r = _run(nc, [arrays], core_ids=[0])
    return r.results[0]["out_0"]
```
